# Optimizing a Trainium2 kernel written in Bass

```python
import numpy as np
import jax
import jax.numpy as jnp

def _softmax(x, axis=-1):
    return jax.nn.softmax(x, axis=axis)

def _gelu(x):
    return jax.nn.gelu(x, approximate=True)

def _silu(x):
    return jax.nn.silu(x)

def _sigmoid(x):
    return jax.nn.sigmoid(x)

def _layernorm(x, axis=-1, eps=1e-05):
    m = jnp.mean(x, axis=axis, keepdims=True)
    v = jnp.var(x, axis=axis, keepdims=True)
    return (x - m) / jnp.sqrt(v + eps)

def _scatter_add(tgt, idx, src, axis=0):
    return tgt.at[idx].add(src)

def _segment_sum(src, seg, n):
    return jax.ops.segment_sum(src, seg, n)
kernel_name = 'mk_rec_standalone_d1_rec_r8_88d6e7'

def setup_inputs(seed: int=0):
    np.random.seed(seed)
    _w = jnp.asarray

    def _rec_inputs():
        import jax
        import jax.numpy as jnp
        _rk = jax.random.key(seed)
        r_visual = 0.000121155 + 1.00018 * jax.random.normal(jax.random.fold_in(_rk, 1), (2048, 256), jnp.float32)
        r_user_id = jax.random.randint(jax.random.fold_in(_rk, 2), (2048,), 79, 999919, jnp.int32)
        r_hour = jax.random.randint(jax.random.fold_in(_rk, 3), (2048,), 0, 24, jnp.int32)
        r_scale = jax.random.uniform(jax.random.fold_in(_rk, 4), (2048, 1), jnp.float32, 0.0, 0.999884)
        r_gender = jax.random.randint(jax.random.fold_in(_rk, 5), (2048,), 0, 2, jnp.int32)
        r_age = jax.random.randint(jax.random.fold_in(_rk, 6), (2048,), 0, 8, jnp.int32)
        r_attribute = jax.random.randint(jax.random.fold_in(_rk, 7), (2048,), 0, 40, jnp.int32)
        return (r_visual, r_user_id, r_hour, r_scale, r_gender, r_age, r_attribute)
    r_visual, r_user_id, r_hour, r_scale, r_gender, r_age, r_attribute = _rec_inputs()

    def _L0_rec_setup():
        import jax, jax.numpy as jnp
        import numpy as np
        NUM_USERS = 125000
        NUM_AGES = 8
        NUM_ATTR = 40
        FACE_K = 64
        VISUAL_DIM = 256
        HIDDEN = 512
        BATCH = 2048
        VOCAB = NUM_USERS + 24 + 2 + NUM_AGES + NUM_ATTR
        key = jax.random.key(seed)
        ks = jax.random.split(key, 24)
        s = 0.02
        inp = {'user_id': jax.random.randint(ks[0], (BATCH,), 0, NUM_USERS), 'hour': jax.random.randint(ks[1], (BATCH,), 0, 24), 'visual': jax.random.normal(ks[2], (BATCH, VISUAL_DIM), jnp.float32), 'scale': jax.random.uniform(ks[3], (BATCH, 1), jnp.float32), 'gender': jax.random.randint(ks[4], (BATCH,), 0, 2), 'age': jax.random.randint(ks[5], (BATCH,), 0, NUM_AGES), 'attribute': jax.random.randint(ks[6], (BATCH,), 0, NUM_ATTR), 'user_emb': jax.random.normal(ks[7], (NUM_USERS, FACE_K), jnp.float32) * s, 'hour_emb': jax.random.normal(ks[8], (24, FACE_K), jnp.float32) * s, 'gender_emb': jax.random.normal(ks[9], (2, FACE_K), jnp.float32) * s, 'age_emb': jax.random.normal(ks[10], (NUM_AGES, FACE_K), jnp.float32) * s, 'attr_emb': jax.random.normal(ks[11], (NUM_ATTR, FACE_K), jnp.float32) * s, 'visu_w': jax.random.normal(ks[12], (FACE_K, VISUAL_DIM), jnp.float32) * s, 'visu_b': jnp.zeros((FACE_K,), jnp.float32), 'fm_w': jax.random.normal(ks[13], (2, VOCAB), jnp.float32) * s, 'fm_b': jnp.zeros((2,), jnp.float32), 'w1': jax.random.normal(ks[14], (HIDDEN, 6 * FACE_K), jnp.float32) * s, 'b1': jnp.zeros((HIDDEN,), jnp.float32), 'w2': jax.random.normal(ks[15], (HIDDEN, HIDDEN), jnp.float32) * s, 'b2': jnp.zeros((HIDDEN,), jnp.float32), 'w3': jax.random.normal(ks[16], (2, HIDDEN), jnp.float32) * s, 'b3': jnp.zeros((2,), jnp.float32)}
        return inp
    _L0_rec_all = _L0_rec_setup()
    _L0_rec_in = {k: v for k, v in _L0_rec_all.items() if k in ('user_emb', 'hour_emb', 'gender_emb', 'age_emb', 'attr_emb', 'visu_w', 'visu_b', 'fm_w', 'fm_b', 'w1', 'b1', 'w2', 'b2', 'w3', 'b3')}
    del _L0_rec_all
    return {'r_visual': r_visual, 'r_user_id': r_user_id, 'r_hour': r_hour, 'r_scale': r_scale, 'r_gender': r_gender, 'r_age': r_age, 'r_attribute': r_attribute, 'L0_rec_user_emb': _L0_rec_in['user_emb'], 'L0_rec_hour_emb': _L0_rec_in['hour_emb'], 'L0_rec_gender_emb': _L0_rec_in['gender_emb'], 'L0_rec_age_emb': _L0_rec_in['age_emb'], 'L0_rec_attr_emb': _L0_rec_in['attr_emb'], 'L0_rec_visu_w': _L0_rec_in['visu_w'], 'L0_rec_visu_b': _L0_rec_in['visu_b'], 'L0_rec_fm_w': _L0_rec_in['fm_w'], 'L0_rec_fm_b': _L0_rec_in['fm_b'], 'L0_rec_w1': _L0_rec_in['w1'], 'L0_rec_b1': _L0_rec_in['b1'], 'L0_rec_w2': _L0_rec_in['w2'], 'L0_rec_b2': _L0_rec_in['b2'], 'L0_rec_w3': _L0_rec_in['w3'], 'L0_rec_b3': _L0_rec_in['b3']}

def reference(r_visual, r_user_id, r_hour, r_scale, r_gender, r_age, r_attribute, L0_rec_user_emb, L0_rec_hour_emb, L0_rec_gender_emb, L0_rec_age_emb, L0_rec_attr_emb, L0_rec_visu_w, L0_rec_visu_b, L0_rec_fm_w, L0_rec_fm_b, L0_rec_w1, L0_rec_b1, L0_rec_w2, L0_rec_b2, L0_rec_w3, L0_rec_b3):
    import jax
    import jax.numpy as jnp

    def _L0_rec_ref(user_id, hour, visual, scale, gender, age, attribute, user_emb, hour_emb, gender_emb, age_emb, attr_emb, visu_w, visu_b, fm_w, fm_b, w1, b1, w2, b2, w3, b3):
        import jax, jax.numpy as jnp
        import numpy as np
        NUM_USERS = 125000
        NUM_AGES = 8
        NUM_ATTR = 40
        FACE_K = 64
        VISUAL_DIM = 256
        HIDDEN = 512
        BATCH = 2048
        VOCAB = NUM_USERS + 24 + 2 + NUM_AGES + NUM_ATTR
        B = user_id.shape[0]
        cols = jnp.stack([user_id, NUM_USERS + hour, NUM_USERS + 24 + gender, NUM_USERS + 24 + 2 + age, NUM_USERS + 24 + 2 + NUM_AGES + attribute], axis=1)
        linear_part = fm_w[:, cols].sum(axis=2).T + fm_b
        user = user_emb[user_id]
        hr = hour_emb[hour]
        face = jnp.stack([gender_emb[gender], attr_emb[attribute], age_emb[age]], axis=1)
        face = scale[:, None, :] * jnp.tanh(face)
        embeddings = jnp.concatenate([user[:, None, :], hr[:, None, :], face], axis=1)
        so = jnp.square(embeddings.sum(axis=1)) - jnp.square(embeddings).sum(axis=1)
        second_order = 0.5 * so.sum(axis=1)
        fm = linear_part + second_order[:, None]
        vis = visual @ visu_w.T + visu_b
        x = jnp.concatenate([embeddings.reshape(B, 5 * FACE_K), vis], axis=1)
        x = jax.nn.relu(x @ w1.T + b1)
        x = jax.nn.relu(x @ w2.T + b2)
        x = x @ w3.T + b3
        return jax.nn.softmax(fm + x, axis=1)
    y = _L0_rec_ref(r_user_id, r_hour, r_visual, r_scale, r_gender, r_age, r_attribute, L0_rec_user_emb, L0_rec_hour_emb, L0_rec_gender_emb, L0_rec_age_emb, L0_rec_attr_emb, L0_rec_visu_w, L0_rec_visu_b, L0_rec_fm_w, L0_rec_fm_b, L0_rec_w1, L0_rec_b1, L0_rec_w2, L0_rec_b2, L0_rec_w3, L0_rec_b3)
    return y

_drawn_inputs = setup_inputs


def setup_inputs(seed=0):
    import zlib

    import numpy as np

    out = dict(_drawn_inputs(seed))
    spreads = {'L0_rec_visu_b': (0.0, 0.8),
     'L0_rec_fm_b': (0.0, 0.662),
     'L0_rec_b1': (0.0, 0.8),
     'L0_rec_b2': (0.0, 2.0),
     'L0_rec_b3': (0.0, 0.697)}
    factors = {'r_visual': 8.0,
     'r_scale': 8.0,
     'L0_rec_user_emb': 24.539,
     'L0_rec_hour_emb': 25.325,
     'L0_rec_gender_emb': 8.0,
     'L0_rec_age_emb': 8.0,
     'L0_rec_attr_emb': 8.0,
     'L0_rec_visu_w': 8.0,
     'L0_rec_w1': 8.0,
     'L0_rec_w2': 8.0,
     'L0_rec_fm_w': 8.0}
    for name, (base, spread) in spreads.items():
        noise = np.random.default_rng([zlib.crc32(name.encode()), seed]).standard_normal(out[name].shape)
        drawn = base * np.exp(spread * noise) if base else spread * noise
        out[name] = jnp.asarray(drawn.astype(out[name].dtype))
    for name, factor in factors.items():
        out[name] = (out[name] * factor).astype(out[name].dtype)
    return out
```

```python
import concourse.bass as bass
from concourse import mybir
from contextlib import ExitStack

P = 128
ROWS = 2048
GROUP = 256
TILES_PER_GROUP = GROUP // P
GROUPS = ROWS // GROUP
TILES = ROWS // P
EMB = 64
VIS = 256
HIDDEN = 512
KT = HIDDEN // P
FIELD_SIZES = (24, 2, 8, 40)
LOOKUP = sum(FIELD_SIZES)
BIAS_ROWS = 2
ROWS_A = LOOKUP + BIAS_ROWS
ROWS_B = LOOKUP - FIELD_SIZES[0]
ROWS_X = ROWS_A + ROWS_B
USERS = 125000
VOCAB = USERS + LOOKUP
FM_COLS = 2 * EMB + 4


def rec_program(nc, visual, user_ids, code_rows, scale_rows, scale_cols, user_emb, fm_user,
                hidden1_w, fold_w, fold_tables, bias_onehot, b1_row, lookup_rows, linear_rows,
                visu_w, visu_b, w2, b2_rows, w3, row_consts, identity, out):
    fp32 = mybir.dt.float32
    fp32r = mybir.dt.float32r
    i32 = mybir.dt.int32
    ALU = mybir.AluOpType
    ACT = mybir.ActivationFunctionType
    AX = mybir.AxisListType.X

    ctx = ExitStack()
    with ctx:
        def sb(name, shape, dt=fp32):
            return ctx.enter_context(nc.sbuf_tensor(name, shape, dt))

        def pb(name, shape, dt=fp32):
            return ctx.enter_context(nc.psum_tensor(name, shape, dt))

        def sem(name):
            return ctx.enter_context(nc.semaphore(name))

        def r(ap):
            return ap.bitcast(fp32r)

        ids = sb("ids", [P, TILES], i32)
        codes = sb("codes", [ROWS_X, ROWS], i32)
        scale_b = sb("scale_b", [ROWS_X, ROWS])
        scale_c = sb("scale_c", [P, TILES])
        vis_in = sb("vis_in", [P, 2, ROWS])
        consts = sb("consts", [P, 5])
        ident = sb("ident", [P, P])
        w1_raw = sb("w1_raw", [P, HIDDEN])
        fold_w_sb = sb("fold_w_sb", [P, 2, HIDDEN])
        fold_t = sb("fold_t", [P, 2, ROWS_X])
        bias_hot = sb("bias_hot", [1, ROWS_X])
        b1_sb = sb("b1_sb", [1, HIDDEN])
        tab = sb("tab", [ROWS_A, FM_COLS])
        visw = sb("visw", [P, 2, EMB])
        visb = sb("visb", [P, 1])
        w2_raw = sb("w2_raw", [P, KT, HIDDEN])
        b2_raw = sb("b2_raw", [2, HIDDEN])
        w3_b = sb("w3_b", [P, 2, HIDDEN])
        w1_hi = sb("w1_hi", [P, HIDDEN])
        w1_lo = sb("w1_lo", [P, HIDDEN])
        w2_hi = sb("w2_hi", [P, KT, HIDDEN])
        w2_lo = sb("w2_lo", [P, KT, HIDDEN])
        fold_hi = sb("fold_hi", [ROWS_X, HIDDEN])
        fold_lo = sb("fold_lo", [ROWS_X, HIDDEN])
        tab_hi = sb("tab_hi", [ROWS_A, FM_COLS])
        tab_lo = sb("tab_lo", [ROWS_A, FM_COLS])
        b2_hi = sb("b2_hi", [2, HIDDEN])
        b2_tmp = sb("b2_tmp", [2, HIDDEN])
        b2_split = sb("b2_split", [2, HIDDEN])
        ones2 = sb("ones2", [2, P])
        id_neg = sb("id_neg", [P, 2, TILES])
        id_wrap = sb("id_wrap", [P, 2, TILES])
        emb_idx = sb("emb_idx", [P, TILES], i32)
        fm_idx = sb("fm_idx", [P, TILES], i32)
        user_rows = sb("user_rows", [P, TILES, EMB])
        fm_rows = sb("fm_rows", [P, TILES, 2])
        user_pad = sb("user_pad", [P, 2, TILES_PER_GROUP, P])
        sc_hi = sb("sc_hi", [ROWS_X, 2, GROUP])
        sc_raw = sb("sc_raw", [ROWS_X, 2, GROUP])
        sc_part = sb("sc_part", [ROWS_X, 2, GROUP])
        hot_scaled = sb("hot_scaled", [ROWS_X, 2, GROUP])
        hot = sb("hot", [ROWS_A, 2, GROUP])
        xa_hi = sb("xa_hi", [P, 2, GROUP])
        xa_lo = sb("xa_lo", [P, 2, GROUP])
        h_hi = sb("h_hi", [P, 2, KT, GROUP])
        h_lo = sb("h_lo", [P, 2, KT, GROUP])
        face_scaled = sb("face_scaled", [P, 2, TILES_PER_GROUP, EMB])
        fm_sum = sb("fm_sum", [P, TILES, EMB])
        fm_small = sb("fm_small", [P, TILES, 4])
        fm_total = sb("fm_total", [P, TILES, EMB])
        fm_sq = sb("fm_sq", [P, TILES, EMB])
        user_sq = sb("user_sq", [P, TILES, EMB])
        sum_sq = sb("sum_sq", [P, TILES])
        user_norm = sb("user_norm", [P, TILES])
        scale2 = sb("scale2", [P, TILES])
        norms = sb("norms", [P, 4, TILES])
        base_lin = sb("base_lin", [P, TILES, 2])
        base = sb("base", [P, TILES, 2])
        dot_sink = sb("dot_sink", [P, 4, 2, HIDDEN])
        mlp = sb("mlp", [P, TILES, 2])
        logits = sb("logits", [P, TILES, 2])
        top = sb("top", [P, TILES])
        shifted = sb("shifted", [P, TILES, 2])
        expd = sb("expd", [P, TILES, 2])
        denom = sb("denom", [P, TILES])
        inv = sb("inv", [P, TILES])
        probs = sb("probs", [P, TILES, 2])

        ps_xa = pb("ps_xa", [P, 512])
        ps_h = [pb(f"ps_h{j}", [P, 2, GROUP]) for j in range(2)]
        ps_fm = pb("ps_fm", [P, 512])
        ps_l2 = [pb(f"ps_l2_{j}", [P, HIDDEN]) for j in range(4)]

        ids_in = sem("ids_in")
        first_in = sem("first_in")
        second_in = sem("second_in")
        rest_in = sem("rest_in")
        vis_first_in = sem("vis_first_in")
        vis_second_in = sem("vis_second_in")
        vis_rest_in = sem("vis_rest_in")
        consts_in = sem("consts_in")
        ident_in = sem("ident_in")
        visw_in = sem("visw_in")
        w1_in = sem("w1_in")
        fold_in = sem("fold_in")
        tab_in = sem("tab_in")
        w2_in = [sem(f"w2_in{k}") for k in range(2)]
        w3_in = sem("w3_in")
        b2_in = sem("b2_in")
        scale_c_in = sem("scale_c_in")
        user_in = [sem(f"user_in{p}") for p in range(2)]
        fm_rows_in = sem("fm_rows_in")
        out_done = sem("out_done")
        dve_step = sem("dve_step")
        act_step = sem("act_step")
        pool_step = sem("pool_step")
        pad_zeroed = sem("pad_zeroed")
        emb_idx_ready = sem("emb_idx_ready")
        fm_idx_ready = sem("fm_idx_ready")
        tables_tanh = sem("tables_tanh")
        fold_done = sem("fold_done")
        fold_hi_done = sem("fold_hi_done")
        fold_lo_done = sem("fold_lo_done")
        w1_hi_done = sem("w1_hi_done")
        w1_lo_done = sem("w1_lo_done")
        w2_hi_done = sem("w2_hi_done")
        w2_lo_done = sem("w2_lo_done")
        tab_hi_done = sem("tab_hi_done")
        tab_lo_done = sem("tab_lo_done")
        b2_parts_done = sem("b2_parts_done")
        b2_done = sem("b2_done")
        ones_done = sem("ones_done")
        pad_ready = sem("pad_ready")
        scale_parts = sem("scale_parts")
        scale_merged = sem("scale_merged")
        hots_ready = sem("hots_ready")
        xa_ready = sem("xa_ready")
        xa_hi_done = sem("xa_hi_done")
        xa_lo_done = sem("xa_lo_done")
        h_ready = sem("h_ready")
        h_hi_done = sem("h_hi_done")
        h_lo_done = sem("h_lo_done")
        fm_ready = sem("fm_ready")
        fm_face_done = sem("fm_face_done")
        fm_taken = sem("fm_taken")
        l2_ready = sem("l2_ready")
        l2_free = sem("l2_free")
        user_norm_done = sem("user_norm_done")
        sum_sq_done = sem("sum_sq_done")
        logits_shifted = sem("logits_shifted")
        exp_done = sem("exp_done")
        probs_done = sem("probs_done")

        LOOP_STEPS = GROUPS - 2
        def in_loop(eng, step):
            with eng.Fori(0, LOOP_STEPS // 2) as i:
                for parity in range(2):
                    step(i * 2 + parity, parity, True, True)
            step(GROUPS - 2, 0, True, False)
            step(GROUPS - 1, 1, False, False)

        def cols(g):
            return bass.ds(g * GROUP, GROUP)

        def tiles(g):
            return bass.ds(g * TILES_PER_GROUP, TILES_PER_GROUP)

        block = ctx.enter_context(nc.Block())

        @block.sync
        def _(sp):
            def rows(lo, hi, arrived):
                sp.dma_start(codes[:, lo:hi], code_rows[:, lo:hi]).then_inc(arrived, 16)
                sp.dma_start(scale_b[:, lo:hi], scale_rows[:, lo:hi]).then_inc(arrived, 16)

            sp.dma_start(ids[:], user_ids).then_inc(ids_in, 16)
            sp.dma_start(consts[:], row_consts).then_inc(consts_in, 16)
            rows(0, GROUP, first_in)
            sp.dma_start(ident[:], identity).then_inc(ident_in, 16)
            sp.dma_start(vis_in[:, :, 0:GROUP], visual[:, :, 0:GROUP]).then_inc(vis_first_in, 16)
            for k in range(2):
                sp.dma_start(w2_raw[:, 2 * k:2 * k + 2, :], w2[:, 2 * k:2 * k + 2, :]).then_inc(w2_in[k], 16)
            rows(GROUP, 2 * GROUP, second_in)
            sp.dma_start(vis_in[:, :, GROUP:2 * GROUP], visual[:, :, GROUP:2 * GROUP]).then_inc(vis_second_in, 16)
            sp.dma_start(w3_b[:], w3.rearrange("(a j) n -> a j n", a=1).to_broadcast([P, 2, HIDDEN])).then_inc(w3_in, 16)
            sp.dma_start(scale_c[:], scale_cols).then_inc(scale_c_in, 16)
            rows(2 * GROUP, ROWS, rest_in)
            sp.dma_start(vis_in[:, :, 2 * GROUP:ROWS], visual[:, :, 2 * GROUP:ROWS]).then_inc(vis_rest_in, 16)
            sp.wait_ge(probs_done, 1)
            sp.dma_start(out, probs[:]).then_inc(out_done, 16)
            sp.wait_ge(out_done, 16)

        @block.gpsimd
        def _(pool):
            nc.gpsimd.memset(user_pad[:], 0.0).then_inc(pad_zeroed, 1)
            pool.wait_ge(emb_idx_ready, 1)
            for t in range(TILES):
                g = t // TILES_PER_GROUP
                if t % TILES_PER_GROUP == 0 and g >= 2:
                    pool.wait_ge(user_in[g % 2], 16 * TILES_PER_GROUP * (g // 2))
                nc.gpsimd.indirect_dma_start(
                    out=user_rows[:, t, :], out_offset=None, in_=user_emb,
                    in_offset=bass.IndirectOffsetOnAxis(ap=emb_idx[:, t:t + 1], axis=0),
                ).then_inc(user_in[g % 2], 16)
            pool.wait_ge(fm_idx_ready, 1)
            for t in range(TILES):
                nc.gpsimd.indirect_dma_start(
                    out=fm_rows[:, t, :], out_offset=None, in_=fm_user,
                    in_offset=bass.IndirectOffsetOnAxis(ap=fm_idx[:, t:t + 1], axis=0),
                ).then_inc(fm_rows_in, 16)
            for p in range(2):
                pool.wait_ge(user_in[p], 16 * TILES // 2)
            nc.gpsimd.tensor_tensor(out=user_sq[:], in0=user_rows[:], in1=user_rows[:],
                                    op=ALU.mult).then_inc(user_norm_done, 1)
            half = TILES // 2
            for n in range(2):
                part = slice(n * half, (n + 1) * half)
                pool.wait_ge(fm_taken, (n + 1) * GROUPS // 2)
                nc.gpsimd.tensor_tensor(out=fm_total[:, part, :], in0=fm_sum[:, part, :],
                                        in1=user_rows[:, part, :], op=ALU.add).then_inc(pool_step, 1)
                pool.wait_ge(pool_step, n + 1)
                nc.gpsimd.tensor_tensor(out=fm_sq[:, part, :], in0=fm_total[:, part, :],
                                        in1=fm_total[:, part, :], op=ALU.mult).then_inc(sum_sq_done, 1)

        @block.scalar
        def _(act):
            act.dma_start(fold_t[:], fold_tables).then_inc(fold_in, 16)
            act.dma_start(fold_w_sb[:], fold_w).then_inc(fold_in, 16)
            act.dma_start(bias_hot[:], bias_onehot).then_inc(fold_in, 16)
            act.dma_start(b1_sb[:], b1_row).then_inc(fold_in, 16)
            act.dma_start(visw[:], visu_w).then_inc(visw_in, 16)
            act.dma_start(visb[:], visu_b).then_inc(visw_in, 16)
            act.dma_start(w1_raw[:], hidden1_w).then_inc(w1_in, 16)
            act.dma_start(tab[:, 0:2 * EMB], lookup_rows).then_inc(tab_in, 16)
            act.dma_start(tab[:, 2 * EMB:2 * EMB + 2], linear_rows).then_inc(tab_in, 16)
            act.dma_start(b2_raw[:], b2_rows).then_inc(b2_in, 16)

            def scale_split(g, parity):
                nc.scalar.activation(r(sc_hi[:, parity, :]), scale_b[:, cols(g)], ACT.Copy)
                nc.scalar.mul(sc_raw[:, parity, :], scale_b[:, cols(g)],
                              consts[0:ROWS_X, 2:3]).then_inc(scale_parts, 1)

            def pad_copy(g, parity):
                act.wait_ge(user_in[parity], pad_level(g, parity))
                nc.scalar.activation(user_pad[:, parity, :, EMB:P], user_rows[:, tiles(g), :],
                                     ACT.Copy).then_inc(pad_ready, 1)

            def pad_level(g, parity):
                return (g - parity) * (16 * TILES_PER_GROUP // 2) + 16 * TILES_PER_GROUP

            act.wait_ge(fold_in, 64)
            nc.scalar.activation(fold_t[EMB:P, 0, :], fold_t[EMB:P, 0, :], ACT.Tanh)
            nc.scalar.activation(fold_t[:, 1, :], fold_t[:, 1, :], ACT.Tanh).then_inc(tables_tanh, 1)
            act.wait_ge(w1_in, 16)
            nc.scalar.activation(r(w1_hi[:]), w1_raw[:], ACT.Copy).then_inc(w1_hi_done, 1)
            act.wait_ge(consts_in, 16)
            act.wait_ge(first_in, 32)
            scale_split(0, 0)
            act.wait_ge(fold_done, 1)
            nc.scalar.activation(r(fold_hi[:]), ps_l2[0][0:ROWS_X, :], ACT.Copy).then_inc(fold_hi_done, 1)
            act.wait_ge(pad_zeroed, 1)
            pad_copy(0, 0)
            act.wait_ge(visw_in, 32)
            act.wait_ge(xa_ready, 1)
            nc.scalar.activation(r(xa_hi[:, 0, :]), ps_xa[:, 0:GROUP], ACT.Identity,
                                 bias=visb[:, 0:1]).then_inc(xa_hi_done, 1)
            for k in range(KT):
                if k % 2 == 0:
                    act.wait_ge(w2_in[k // 2], 16)
                nc.scalar.activation(r(w2_hi[:, k, :]), w2_raw[:, k, :], ACT.Copy).then_inc(w2_hi_done, 1)
            act.wait_ge(b2_in, 16)
            nc.scalar.activation(r(b2_hi[:]), b2_raw[:], ACT.Copy)
            nc.scalar.mul(b2_tmp[:], b2_raw[:], consts[0:2, 4:5]).then_inc(b2_parts_done, 1)
            act.wait_ge(tab_in, 32)
            nc.scalar.activation(tab[:, EMB:2 * EMB], tab[:, EMB:2 * EMB], ACT.Tanh).then_inc(act_step, 1)
            act.wait_ge(act_step, 1)
            nc.scalar.activation(dot_sink[0:ROWS_A, 3, 0, 0:EMB], tab[:, 0:EMB], ACT.Square,
                                 accum_out=tab[:, 2 * EMB + 2:2 * EMB + 3])
            nc.scalar.activation(dot_sink[0:ROWS_A, 3, 1, 0:EMB], tab[:, EMB:2 * EMB], ACT.Square,
                                 accum_out=tab[:, 2 * EMB + 3:2 * EMB + 4]).then_inc(act_step, 1)
            act.wait_ge(act_step, 2)
            nc.scalar.activation(r(tab_hi[:]), tab[:], ACT.Copy).then_inc(tab_hi_done, 1)
            act.wait_ge(second_in, 32)
            scale_split(1, 1)
            pad_copy(1, 1)

            def hidden_hi(g, parity):
                for j in range(2):
                    act.wait_ge(h_ready, g * 2 + j + 1)
                    nc.scalar.activation(r(h_hi[:, parity, 2 * j:2 * j + 2, :]), ps_h[j][:],
                                         ACT.Relu).then_inc(h_hi_done, 1)

            hidden_hi(0, 0)

            def step(g, parity, front, codes_ahead):
                if not front:
                    return
                nxt = 1 - parity
                act.wait_ge(xa_ready, g + 2)
                nc.scalar.activation(r(xa_hi[:, nxt, :]), ps_xa[:, 0:GROUP], ACT.Identity,
                                     bias=visb[:, 0:1]).then_inc(xa_hi_done, 1)
                if codes_ahead:
                    pad_copy(g + 2, parity)
                    act.wait_ge(rest_in, 32)
                    act.wait_ge(scale_merged, g + 1)
                    scale_split(g + 2, parity)
                hidden_hi(g + 1, nxt)

            in_loop(act, step)
            act.wait_ge(logits_shifted, 1)
            nc.scalar.activation(expd[:], shifted[:], ACT.Exp).then_inc(exp_done, 1)

        @block.vector
        def _(dve):
            linked = [0]

            def link(ins):
                linked[0] += 1
                ins.then_inc(dve_step, 1)
                dve.wait_ge(dve_step, linked[0])

            dve.wait_ge(ids_in, 16)
            for n, size in enumerate((USERS, VOCAB)):
                last = nc.vector.tensor_scalar(id_neg[:, n, :], ids[:], 0.0, float(size), ALU.is_lt, ALU.mult)
            link(last)
            for n in range(2):
                last = nc.vector.tensor_tensor(id_wrap[:, n, :], id_neg[:, n, :], ids[:], ALU.add)
            link(last)
            nc.vector.tensor_scalar(emb_idx[:], id_wrap[:, 0, :], 0.0, float(USERS - 1), ALU.max,
                                    ALU.min).then_inc(emb_idx_ready, 1)
            nc.vector.tensor_scalar(fm_idx[:], id_wrap[:, 1, :], 0.0, float(VOCAB - 1), ALU.max,
                                    ALU.min).then_inc(fm_idx_ready, 1)
            nc.vector.memset(ones2[:], 1.0).then_inc(ones_done, 1)
            nc.vector.memset(inv[:], 0.0).then_inc(l2_free, 4)

            def make_hots(g, parity):
                dve.wait_ge(scale_parts, g + 1)
                nc.vector.scalar_tensor_tensor(out=sc_part[:, parity, :], in0=sc_hi[:, parity, :],
                                               scalar=consts[0:ROWS_X, 1:2], in1=sc_raw[:, parity, :],
                                               op0=ALU.mult, op1=ALU.add).then_inc(scale_merged, 1)
                nc.vector.tensor_scalar(r(hot[:, parity, :]), codes[0:ROWS_A, cols(g)],
                                        consts[0:ROWS_A, 0:1], None, ALU.is_equal)
                dve.wait_ge(scale_merged, g + 1)
                nc.vector.scalar_tensor_tensor(out=r(hot_scaled[:, parity, :]), in0=codes[:, cols(g)],
                                               scalar=consts[0:ROWS_X, 0:1], in1=sc_part[:, parity, :],
                                               op0=ALU.is_equal, op1=ALU.mult).then_inc(hots_ready, 1)

            def inputs_lo(g, parity):
                dve.wait_ge(xa_hi_done, g + 1)
                nc.vector.scalar_tensor_tensor(out=r(xa_lo[:, parity, :]), in0=ps_xa[:, 0:GROUP],
                                               scalar=visb[:, 0:1], in1=xa_hi[:, parity, :],
                                               op0=ALU.add, op1=ALU.subtract).then_inc(xa_lo_done, 1)

            def hidden_lo(g, parity):
                for j in range(2):
                    dve.wait_ge(h_hi_done, g * 2 + j + 1)
                    nc.vector.scalar_tensor_tensor(out=r(h_lo[:, parity, 2 * j:2 * j + 2, :]), in0=ps_h[j][:],
                                                   scalar=0.0, in1=h_hi[:, parity, 2 * j:2 * j + 2, :],
                                                   op0=ALU.max, op1=ALU.subtract).then_inc(h_lo_done, 1)

            def fm_take(g, parity):
                dve.wait_ge(fm_ready, g + 1)
                ps = ps_fm[:, 0:TILES_PER_GROUP * FM_COLS].rearrange("p (t c) -> p t c", c=FM_COLS)
                nc.vector.tensor_copy(fm_small[:, tiles(g), :], ps[:, :, 2 * EMB:FM_COLS])
                for t in range(TILES_PER_GROUP):
                    last = nc.vector.tensor_scalar(face_scaled[:, parity, t, :], ps[:, t, EMB:2 * EMB],
                                                   scale_c[:, bass.ds(g * TILES_PER_GROUP + t, 1)], None, ALU.mult)
                last.then_inc(fm_face_done, 1)
                dve.wait_ge(fm_face_done, g + 1)
                nc.vector.tensor_tensor(out=fm_sum[:, tiles(g), :], in0=ps[:, :, 0:EMB],
                                        in1=face_scaled[:, parity, :, :], op=ALU.add).then_inc(fm_taken, 1)

            def output_dots(g, parity, t):
                dve.wait_ge(l2_ready, g * 2 + t + 1)
                dve.wait_ge(l2_free, g * 2 + t + 1)
                for j in range(2):
                    last = nc.vector.scalar_tensor_tensor(
                        out=dot_sink[:, 2 * parity + t, j, :], in0=ps_l2[2 * parity + t][:], scalar=0.0, in1=w3_b[:, j, :],
                        op0=ALU.max, op1=ALU.mult, accum_out=mlp[:, bass.ds(g * 2 + t, 1), j])
                last.then_inc(l2_free, 1)

            dve.wait_ge(consts_in, 16)
            dve.wait_ge(first_in, 32)
            make_hots(0, 0)
            dve.wait_ge(w1_hi_done, 1)
            nc.vector.tensor_tensor(r(w1_lo[:]), w1_raw[:], w1_hi[:], ALU.subtract).then_inc(w1_lo_done, 1)
            dve.wait_ge(fold_hi_done, 1)
            nc.vector.tensor_tensor(r(fold_lo[:]), ps_l2[0][0:ROWS_X, :], fold_hi[:],
                                    ALU.subtract).then_inc(fold_lo_done, 1)
            dve.wait_ge(visw_in, 32)
            inputs_lo(0, 0)
            for k in range(KT):
                dve.wait_ge(w2_hi_done, k + 1)
                nc.vector.tensor_tensor(r(w2_lo[:, k, :]), w2_raw[:, k, :], w2_hi[:, k, :],
                                        ALU.subtract).then_inc(w2_lo_done, 1)
            dve.wait_ge(b2_parts_done, 1)
            nc.vector.scalar_tensor_tensor(out=r(b2_split[:]), in0=b2_hi[:], scalar=consts[0:2, 3:4],
                                           in1=b2_tmp[:], op0=ALU.mult, op1=ALU.add).then_inc(b2_done, 1)
            dve.wait_ge(tab_hi_done, 1)
            nc.vector.tensor_tensor(r(tab_lo[:]), tab[:], tab_hi[:], ALU.subtract).then_inc(tab_lo_done, 1)
            hidden_lo(0, 0)
            dve.wait_ge(second_in, 32)
            make_hots(1, 1)
            dve.wait_ge(scale_c_in, 16)
            fm_take(0, 0)
            dve.wait_ge(w3_in, 16)

            def step(g, parity, front, codes_ahead):
                nxt = 1 - parity
                if front:
                    inputs_lo(g + 1, nxt)
                    if codes_ahead:
                        dve.wait_ge(rest_in, 32)
                        dve.wait_ge(fm_ready, g + 1)
                        make_hots(g + 2, parity)
                output_dots(g, parity, 0)
                if front:
                    hidden_lo(g + 1, nxt)
                    fm_take(g + 1, nxt)
                output_dots(g, parity, 1)

            with dve.Fori(0, LOOP_STEPS // 2) as i:
                for parity in range(2):
                    step(i * 2 + parity, parity, True, True)
            step(GROUPS - 2, 0, True, False)

            dve.wait_ge(user_norm_done, 1)
            nc.vector.reduce_sum(user_norm[:], user_sq[:], axis=AX)
            nc.vector.tensor_tensor(scale2[:], scale_c[:], scale_c[:], ALU.mult)
            dve.wait_ge(fm_rows_in, 16 * TILES)
            dve.wait_ge(fm_taken, GROUPS)
            nc.vector.tensor_tensor(base_lin[:], fm_small[:, :, 0:2], fm_rows[:], ALU.add)
            dve.wait_ge(sum_sq_done, 2)
            link(nc.vector.reduce_sum(sum_sq[:], fm_sq[:], axis=AX))
            nc.vector.tensor_tensor(norms[:, 0, :], user_norm[:], fm_small[:, :, 2], ALU.add)
            link(nc.vector.tensor_tensor(norms[:, 1, :], scale2[:], fm_small[:, :, 3], ALU.mult))
            link(nc.vector.tensor_tensor(norms[:, 2, :], norms[:, 0, :], norms[:, 1, :], ALU.add))
            link(nc.vector.tensor_tensor(norms[:, 3, :], sum_sq[:], norms[:, 2, :], ALU.subtract))
            for j in range(2):
                last = nc.vector.scalar_tensor_tensor(out=base[:, :, j], in0=norms[:, 3, :], scalar=0.5,
                                                      in1=base_lin[:, :, j], op0=ALU.mult, op1=ALU.add)
            link(last)
            step(GROUPS - 1, 1, False, False)

            dve.wait_ge(l2_free, 4 + TILES)
            link(nc.vector.tensor_tensor(logits[:], mlp[:], base[:], ALU.add))
            link(nc.vector.tensor_tensor(top[:], logits[:, :, 0], logits[:, :, 1], ALU.max))
            for j in range(2):
                last = nc.vector.tensor_tensor(shifted[:, :, j], logits[:, :, j], top[:], ALU.subtract)
            last.then_inc(logits_shifted, 1)
            dve.wait_ge(exp_done, 1)
            link(nc.vector.tensor_tensor(denom[:], expd[:, :, 0], expd[:, :, 1], ALU.add))
            link(nc.vector.reciprocal(inv[:], denom[:]))
            for j in range(2):
                last = nc.vector.tensor_tensor(probs[:, :, j], expd[:, :, j], inv[:], ALU.mult)
            last.then_inc(probs_done, 1)

        @block.tensor
        def _(pe):
            def front(g, parity):
                pe.wait_ge(pad_ready, g + 1)
                for t in range(TILES_PER_GROUP):
                    nc.tensor.transpose(ps_xa[:, t * P:(t + 1) * P], user_pad[:, parity, t, :], ident[:])
                for k in range(2):
                    last = nc.tensor.matmul(ps_xa[0:EMB, 0:GROUP], visw[:, k, :], vis_in[:, k, cols(g)],
                                            start=(k == 0), stop=(k == 1))
                last.then_inc(xa_ready, 1)

            def layer1(g, parity):
                pe.wait_ge(hots_ready, g + 1)
                pe.wait_ge(xa_lo_done, g + 1)
                for m in range(KT):
                    o = ps_h[m // 2][:, m % 2, :]
                    mc = slice(m * P, (m + 1) * P)
                    nc.tensor.matmul(o, r(fold_hi[:, mc]), r(hot_scaled[:, parity, :]), start=True, stop=False)
                    nc.tensor.matmul(o, r(fold_lo[0:ROWS_A, mc]), r(hot_scaled[0:ROWS_A, parity, :]),
                                     start=False, stop=False)
                    nc.tensor.matmul(o, r(w1_hi[:, mc]), r(xa_hi[:, parity, :]), start=False, stop=False)
                    nc.tensor.matmul(o, r(w1_lo[:, mc]), r(xa_hi[:, parity, :]), start=False, stop=False)
                    last = nc.tensor.matmul(o, r(w1_hi[:, mc]), r(xa_lo[:, parity, :]), start=False, stop=True)
                    if m % 2 == 1:
                        last.then_inc(h_ready, 1)

            def lookups(g, parity):
                for t in range(TILES_PER_GROUP):
                    o = ps_fm[:, t * FM_COLS:(t + 1) * FM_COLS]
                    h = r(hot[:, parity, t * P:(t + 1) * P])
                    nc.tensor.matmul(o, h, r(tab_hi[:]), start=True, stop=False)
                    last = nc.tensor.matmul(o, h, r(tab_lo[:]), start=False, stop=True)
                last.then_inc(fm_ready, 1)

            def layer2(g, parity, t):
                pe.wait_ge(l2_free, g * 2 + t + 1)
                o = ps_l2[2 * parity + t][:]
                tc = slice(t * P, (t + 1) * P)
                nc.tensor.matmul(o, r(ones2[:]), r(b2_split[:]), start=True, stop=False)
                for k in range(KT):
                    if t == 0 and k % 2 == 0:
                        pe.wait_ge(h_lo_done, g * 2 + k // 2 + 1)
                    hi = r(h_hi[:, parity, k, tc])
                    lo = r(h_lo[:, parity, k, tc])
                    nc.tensor.matmul(o, hi, r(w2_hi[:, k, :]), start=False, stop=False)
                    nc.tensor.matmul(o, hi, r(w2_lo[:, k, :]), start=False, stop=False)
                    last = nc.tensor.matmul(o, lo, r(w2_hi[:, k, :]), start=False, stop=(k == KT - 1))
                last.then_inc(l2_ready, 1)

            pe.wait_ge(tables_tanh, 1)
            o = ps_l2[0][0:ROWS_X, :]
            for n in range(2):
                nc.tensor.matmul(o, fold_t[:, n, :], fold_w_sb[:, n, :], start=(n == 0), stop=False)
            nc.tensor.matmul(o, bias_hot[:], b1_sb[:], start=False, stop=True).then_inc(fold_done, 1)
            pe.wait_ge(ident_in, 16)
            pe.wait_ge(visw_in, 32)
            pe.wait_ge(vis_first_in, 16)
            front(0, 0)
            pe.wait_ge(fold_lo_done, 1)
            pe.wait_ge(w1_lo_done, 1)
            layer1(0, 0)
            pe.wait_ge(tab_lo_done, 1)
            lookups(0, 0)
            pe.wait_ge(vis_second_in, 16)
            pe.wait_ge(ones_done, 1)
            pe.wait_ge(b2_done, 1)
            pe.wait_ge(w2_lo_done, KT)

            def step(g, parity, front_too, _):
                nxt = 1 - parity
                if front_too:
                    if parity == 1:
                        pe.wait_ge(vis_rest_in, 16)
                    front(g + 1, nxt)
                layer2(g, parity, 0)
                if front_too:
                    layer1(g + 1, nxt)
                    pe.wait_ge(fm_taken, g + 1)
                    lookups(g + 1, nxt)
                layer2(g, parity, 1)

            in_loop(pe, step)


def kernel(r_visual, r_user_id, r_hour, r_scale, r_gender, r_age, r_attribute, L0_rec_user_emb,
           L0_rec_hour_emb, L0_rec_gender_emb, L0_rec_age_emb, L0_rec_attr_emb, L0_rec_visu_w,
           L0_rec_visu_b, L0_rec_fm_w, L0_rec_fm_b, L0_rec_w1, L0_rec_b1, L0_rec_w2, L0_rec_b2,
           L0_rec_w3, L0_rec_b3):
    import numpy as np
    import concourse.bacc as bacc
    from concourse.bass_utils import run_bass_kernel_spmd

    f32 = np.float32
    visual = np.asarray(r_visual).T.reshape(2, P, ROWS).transpose(1, 0, 2)
    by_tile = lambda a: np.asarray(a).reshape(TILES, P).T

    ids = [np.asarray(a)[None, :] for a in (r_hour, r_gender, r_age, r_attribute)]
    repeated = [np.repeat(a, n, axis=0) for a, n in zip(ids, FIELD_SIZES)]
    code_rows = np.concatenate(repeated + [np.zeros((BIAS_ROWS, ROWS), ids[0].dtype)] + repeated[1:])
    scale = np.asarray(r_scale).reshape(1, ROWS)
    scale_rows = np.concatenate([np.ones((FIELD_SIZES[0], ROWS), f32), np.repeat(scale, ROWS_B, axis=0),
                                 np.ones((BIAS_ROWS, ROWS), f32), np.repeat(scale, ROWS_B, axis=0)])

    numbers = [np.arange(n) for n in FIELD_SIZES]
    row_consts = np.zeros((P, 5), f32)
    row_consts[0:ROWS_X, 0] = np.concatenate(numbers + [np.zeros(BIAS_ROWS)] + numbers[1:])
    row_consts[0:ROWS_A, 1] = 1.0
    row_consts[ROWS_A:ROWS_X, 1] = -1.0
    row_consts[ROWS_A:ROWS_X, 2] = 1.0
    row_consts[0:2, 3] = (1.0, -1.0)
    row_consts[0:2, 4] = (0.0, 1.0)

    w1t = np.asarray(L0_rec_w1).T
    user_w, hour_w, gender_w, attr_w, age_w, vis_w = (w1t[n * EMB:(n + 1) * EMB] for n in range(6))
    hidden1_w = np.concatenate([vis_w, user_w])
    fold_w = np.stack([np.concatenate([hour_w, age_w]), np.concatenate([gender_w, attr_w])], axis=1)
    hour, gender, age, attr = (np.asarray(a) for a in (L0_rec_hour_emb, L0_rec_gender_emb,
                                                       L0_rec_age_emb, L0_rec_attr_emb))
    starts = np.cumsum((0,) + FIELD_SIZES)
    fold_tables = np.zeros((P, 2, ROWS_X), f32)
    lookup_rows = np.zeros((ROWS_A, 2 * EMB), f32)
    for n, (table, place) in enumerate(((hour, (0, 0)), (gender, (0, 1)), (age, (EMB, 0)), (attr, (EMB, 1)))):
        top, pair = place
        at = starts[n]
        fold_tables[top:top + EMB, pair, at:at + len(table)] = table.T
        lookup_rows[at:at + len(table), (0 if n == 0 else EMB):][:, :EMB] = table
        if n:
            at += ROWS_A - FIELD_SIZES[0]
            fold_tables[top:top + EMB, pair, at:at + len(table)] = table.T
    bias_onehot = np.zeros((1, ROWS_X), f32)
    bias_onehot[0, LOOKUP] = 1.0
    fm_rows = np.asarray(L0_rec_fm_w).T
    linear_rows = np.concatenate([fm_rows[USERS:], np.asarray(L0_rec_fm_b)[None, :], np.asarray(L0_rec_b3)[None, :]])

    arrays = {
        "visual": visual,
        "user_ids": by_tile(r_user_id),
        "code_rows": code_rows,
        "scale_rows": scale_rows,
        "scale_cols": by_tile(r_scale),
        "user_emb": L0_rec_user_emb,
        "fm_user": fm_rows,
        "hidden1_w": hidden1_w,
        "fold_w": fold_w,
        "fold_tables": fold_tables,
        "bias_onehot": bias_onehot,
        "b1_row": np.asarray(L0_rec_b1)[None, :],
        "lookup_rows": lookup_rows,
        "linear_rows": linear_rows,
        "visu_w": np.asarray(L0_rec_visu_w).T.reshape(2, P, EMB).transpose(1, 0, 2),
        "visu_b": np.concatenate([np.asarray(L0_rec_visu_b), np.zeros(EMB, f32)])[:, None],
        "w2": np.asarray(L0_rec_w2).T.reshape(KT, P, HIDDEN).transpose(1, 0, 2),
        "b2_rows": np.repeat(np.asarray(L0_rec_b2)[None, :], 2, axis=0),
        "w3": L0_rec_w3,
        "row_consts": row_consts,
        "identity": np.eye(P, dtype=f32),
    }
    arrays = {name: np.ascontiguousarray(a) for name, a in arrays.items()}
    nc = bacc.Bacc("TRN2", target_bir_lowering=False, num_devices=1)
    aps = [nc.dram_tensor(name, a.shape, mybir.dt.from_np(a.dtype), kind="ExternalInput").ap()
           for name, a in arrays.items()]
    out = nc.dram_tensor("out", (P, TILES, 2), mybir.dt.float32, kind="ExternalOutput").ap()
    rec_program(nc, *aps, out)
    result = run_bass_kernel_spmd(nc, [arrays], core_ids=[0])
    return result.results[0]["out"].transpose(1, 0, 2).reshape(ROWS, 2)
```

```python
import concourse.bass as bass
from concourse import mybir
from contextlib import ExitStack

P = 128
ROWS = 2048
GROUP = 256
TILES_PER_GROUP = GROUP // P
GROUPS = ROWS // GROUP
TILES = ROWS // P
EMB = 64
VIS = 256
HIDDEN = 512
KT = HIDDEN // P
FIELD_SIZES = (24, 2, 8, 40)
LOOKUP = sum(FIELD_SIZES)
BIAS_ROWS = 2
ROWS_A = LOOKUP + BIAS_ROWS
ROWS_B = LOOKUP - FIELD_SIZES[0]
ROWS_X = ROWS_A + ROWS_B
USERS = 125000
VOCAB = USERS + LOOKUP
WARM_UP = (10, 5, 3)
FM_COLS = 2 * EMB + 4


FOLD_COLS = 2 * ROWS_X
CONST_COLS = 3
VISW_COLS = 2 * EMB
SMALL_EARLY = FOLD_COLS + CONST_COLS
SMALL_LATE = VISW_COLS + 1 + P


def rec_program(nc, visual, user_ids, lookup_inputs, scale_cols, user_emb, fm_user, hidden1_w, fold_w,
                small_early, small_late, b1_row, lookup_tables, w2, out_rows, out):
    fp32 = mybir.dt.float32
    fp32r = mybir.dt.float32r
    i32 = mybir.dt.int32
    ALU = mybir.AluOpType
    ACT = mybir.ActivationFunctionType
    AX = mybir.AxisListType.X

    ctx = ExitStack()
    with ctx:
        def sb(name, shape, dt=fp32):
            return ctx.enter_context(nc.sbuf_tensor(name, shape, dt))

        def pb(name, shape, dt=fp32):
            return ctx.enter_context(nc.psum_tensor(name, shape, dt))

        def sem(name):
            return ctx.enter_context(nc.semaphore(name))

        def r(ap):
            return ap.bitcast(fp32r)

        ids = sb("ids", [P, TILES], i32)
        lookup_in = sb("lookup_in", [ROWS_X, 2, ROWS], i32)
        codes = lookup_in[:, 0, :]
        scale_b = lookup_in[:, 1, :].bitcast(fp32)
        scale_c = sb("scale_c", [P, TILES])
        vis_in = sb("vis_in", [P, 2, ROWS])
        early = sb("early", [P, SMALL_EARLY])
        late = sb("late", [P, SMALL_LATE])
        fold_t = early[:, 0:FOLD_COLS].rearrange("p (n r) -> p n r", n=2)
        consts = early[:, FOLD_COLS:SMALL_EARLY]
        visw = late[:, 0:VISW_COLS].rearrange("p (k d) -> p k d", k=2)
        visb = late[:, VISW_COLS:VISW_COLS + 1]
        ident = late[:, VISW_COLS + 1:SMALL_LATE]
        b1_sb = sb("b1_sb", [1, HIDDEN + ROWS_X])
        w1_raw = sb("w1_raw", [P, HIDDEN])
        fold_w_sb = sb("fold_w_sb", [P, 2, HIDDEN])
        tab = sb("tab", [ROWS_A, FM_COLS])
        w2_raw = sb("w2_raw", [P, KT, HIDDEN])
        out_b = sb("out_b", [P, 3, HIDDEN])
        b2_b = out_b[:, 0, :]
        w3_b = out_b[:, 1:3, :]
        warm = sb("warm", [P, HIDDEN], mybir.dt.bfloat16)
        w1_hi = sb("w1_hi", [P, HIDDEN])
        w1_lo = sb("w1_lo", [P, HIDDEN])
        w2_hi = sb("w2_hi", [P, KT, HIDDEN])
        w2_lo = sb("w2_lo", [P, KT, HIDDEN])
        fold_hi = sb("fold_hi", [ROWS_X, HIDDEN])
        fold_lo = sb("fold_lo", [ROWS_X, HIDDEN])
        norm_sink = sb("norm_sink", [ROWS_A, 2, EMB])
        tab_hi = sb("tab_hi", [ROWS_A, FM_COLS])
        tab_lo = sb("tab_lo", [ROWS_A, FM_COLS])
        id_neg = sb("id_neg", [P, 2, TILES])
        id_wrap = sb("id_wrap", [P, 2, TILES])
        emb_idx = sb("emb_idx", [P, TILES], i32)
        fm_idx = sb("fm_idx", [P, TILES], i32)
        user_rows = sb("user_rows", [P, TILES, EMB])
        fm_rows = sb("fm_rows", [P, TILES, 2])
        user_pad = sb("user_pad", [P, 2, TILES_PER_GROUP, P])
        sc_hi = sb("sc_hi", [ROWS_X, 2, GROUP])
        sc_raw = sb("sc_raw", [ROWS_X, 2, GROUP])
        sc_part = sb("sc_part", [ROWS_X, 2, GROUP])
        hot_scaled = sb("hot_scaled", [ROWS_X, 2, GROUP])
        hot = sb("hot", [ROWS_A, 2, GROUP])
        xa_hi = sb("xa_hi", [P, 2, GROUP])
        xa_lo = sb("xa_lo", [P, 2, GROUP])
        h_hi = sb("h_hi", [P, 2, KT, GROUP])
        h_lo = sb("h_lo", [P, 2, KT, GROUP])
        face_scaled = sb("face_scaled", [P, 2, TILES_PER_GROUP, EMB])
        fm_sum = sb("fm_sum", [P, TILES, EMB])
        fm_small = sb("fm_small", [P, TILES, 4])
        fm_total = sb("fm_total", [P, TILES, EMB])
        fm_sq = sb("fm_sq", [P, TILES, EMB])
        user_sq = sb("user_sq", [P, TILES, EMB])
        sum_sq = sb("sum_sq", [P, TILES])
        user_norm = sb("user_norm", [P, TILES])
        scale2 = sb("scale2", [P, TILES])
        norms = sb("norms", [P, 4, TILES])
        base_lin = sb("base_lin", [P, TILES, 2])
        base = sb("base", [P, TILES, 2])
        hidden2 = sb("hidden2", [P, 4, HIDDEN])
        dot_sink = sb("dot_sink", [P, 4, 2, HIDDEN])
        mlp = sb("mlp", [P, TILES, 2])
        logits = sb("logits", [P, TILES, 2])
        top = sb("top", [P, TILES])
        shifted = sb("shifted", [P, TILES, 2])
        expd = sb("expd", [P, TILES, 2])
        denom = sb("denom", [P, TILES])
        inv = sb("inv", [P, TILES])
        probs = sb("probs", [P, TILES, 2])

        ps_xa = pb("ps_xa", [P, 512])
        ps_h = [pb(f"ps_h{j}", [P, 2, GROUP]) for j in range(2)]
        ps_fm = pb("ps_fm", [P, 512])
        ps_l2 = [pb(f"ps_l2_{j}", [P, HIDDEN]) for j in range(4)]

        ids_in = sem("ids_in")
        first_in = sem("first_in")
        second_in = sem("second_in")
        rest_in = sem("rest_in")
        vis_first_in = sem("vis_first_in")
        vis_second_in = sem("vis_second_in")
        vis_rest_in = sem("vis_rest_in")
        early_in = sem("early_in")
        late_in = sem("late_in")
        w1_in = sem("w1_in")
        fold_in = sem("fold_in")
        tab_in = sem("tab_in")
        w2_in = [sem(f"w2_in{k}") for k in range(2)]
        out_rows_in = sem("out_rows_in")
        b1_in = sem("b1_in")
        scale_c_in = sem("scale_c_in")
        user_in = [sem(f"user_in{p}") for p in range(2)]
        fm_rows_in = sem("fm_rows_in")
        out_done = sem("out_done")
        dve_step = sem("dve_step")
        act_step = sem("act_step")
        pool_step = sem("pool_step")
        pad_zeroed = sem("pad_zeroed")
        emb_idx_ready = sem("emb_idx_ready")
        fm_idx_ready = sem("fm_idx_ready")
        tables_tanh = sem("tables_tanh")
        fold_done = sem("fold_done")
        fold_hi_done = sem("fold_hi_done")
        fold_lo_done = sem("fold_lo_done")
        w1_hi_done = sem("w1_hi_done")
        w1_lo_done = sem("w1_lo_done")
        w2_hi_done = sem("w2_hi_done")
        w2_lo_done = sem("w2_lo_done")
        tab_hi_done = sem("tab_hi_done")
        tab_lo_done = sem("tab_lo_done")
        warm_zeroed = sem("warm_zeroed")
        dots_done = sem("dots_done")
        pad_ready = sem("pad_ready")
        scale_parts = sem("scale_parts")
        scale_merged = sem("scale_merged")
        hots_ready = sem("hots_ready")
        xa_ready = sem("xa_ready")
        xa_hi_done = sem("xa_hi_done")
        xa_lo_done = sem("xa_lo_done")
        h_ready = sem("h_ready")
        h_hi_done = sem("h_hi_done")
        h_lo_done = sem("h_lo_done")
        fm_ready = sem("fm_ready")
        fm_face_done = sem("fm_face_done")
        fm_taken = sem("fm_taken")
        l2_ready = sem("l2_ready")
        l2_free = sem("l2_free")
        user_norm_done = sem("user_norm_done")
        sum_sq_done = sem("sum_sq_done")
        logits_shifted = sem("logits_shifted")
        exp_done = sem("exp_done")
        probs_done = sem("probs_done")

        LOOP_STEPS = GROUPS - 2
        def cols(g):
            return bass.ds(g * GROUP, GROUP)

        def tiles(g):
            return bass.ds(g * TILES_PER_GROUP, TILES_PER_GROUP)

        block = ctx.enter_context(nc.Block())

        @block.sync
        def _(sp):
            def rows(lo, hi, arrived, vis_arrived):
                sp.dma_start(lookup_in[:, :, lo:hi], lookup_inputs[:, :, lo:hi]).then_inc(arrived, 16)
                sp.dma_start(vis_in[:, :, lo:hi], visual[:, :, lo:hi]).then_inc(vis_arrived, 16)

            sp.dma_start(ids[:], user_ids).then_inc(ids_in, 16)
            sp.dma_start(early[:], small_early).then_inc(early_in, 16)
            sp.dma_start(fold_w_sb[:], fold_w).then_inc(fold_in, 16)
            sp.dma_start(b1_sb[:], b1_row).then_inc(b1_in, 16)
            sp.dma_start(late[:], small_late).then_inc(late_in, 16)
            rows(0, GROUP, first_in, vis_first_in)
            sp.dma_start(w1_raw[:], hidden1_w).then_inc(w1_in, 16)
            rows(GROUP, 2 * GROUP, second_in, vis_second_in)
            for k in range(2):
                sp.dma_start(w2_raw[:, 2 * k:2 * k + 2, :], w2[:, 2 * k:2 * k + 2, :]).then_inc(w2_in[k], 16)
            sp.dma_start(tab[:, 0:2 * EMB + 2], lookup_tables).then_inc(tab_in, 16)
            sp.dma_start(scale_c[:], scale_cols).then_inc(scale_c_in, 16)
            sp.dma_start(out_b[:], out_rows.rearrange("(a j) n -> a j n", a=1)
                         .to_broadcast([P, 3, HIDDEN])).then_inc(out_rows_in, 16)
            for pair in range(1, GROUPS // 2):
                if pair > 1:
                    sp.wait_ge(rest_in, 16 * (pair - 1))
                    sp.wait_ge(vis_rest_in, 16 * (pair - 1))
                rows(pair * 2 * GROUP, (pair + 1) * 2 * GROUP, rest_in, vis_rest_in)
            sp.wait_ge(probs_done, 1)
            sp.dma_start(out, probs[:]).then_inc(out_done, 16)
            sp.wait_ge(out_done, 16)

        @block.gpsimd
        def _(pool):
            nc.gpsimd.memset(user_pad[:], 0.0).then_inc(pad_zeroed, 1)
            pool.wait_ge(emb_idx_ready, 1)
            for t in range(TILES):
                g = t // TILES_PER_GROUP
                if t % TILES_PER_GROUP == 0 and g >= 2:
                    pool.wait_ge(user_in[g % 2], 16 * TILES_PER_GROUP * (g // 2))
                nc.gpsimd.indirect_dma_start(
                    out=user_rows[:, t, :], out_offset=None, in_=user_emb,
                    in_offset=bass.IndirectOffsetOnAxis(ap=emb_idx[:, t:t + 1], axis=0),
                ).then_inc(user_in[g % 2], 16)
            pool.wait_ge(fm_idx_ready, 1)
            for t in range(TILES):
                nc.gpsimd.indirect_dma_start(
                    out=fm_rows[:, t, :], out_offset=None, in_=fm_user,
                    in_offset=bass.IndirectOffsetOnAxis(ap=fm_idx[:, t:t + 1], axis=0),
                ).then_inc(fm_rows_in, 16)
            for p in range(2):
                pool.wait_ge(user_in[p], 16 * TILES // 2)
            nc.gpsimd.tensor_tensor(out=user_sq[:], in0=user_rows[:], in1=user_rows[:],
                                    op=ALU.mult).then_inc(user_norm_done, 1)
            done = 0
            for n, groups in enumerate((GROUPS - 2, GROUPS)):
                part = slice(done * TILES_PER_GROUP, groups * TILES_PER_GROUP)
                done = groups
                pool.wait_ge(fm_taken, groups + 1)
                nc.gpsimd.tensor_tensor(out=fm_total[:, part, :], in0=fm_sum[:, part, :],
                                        in1=user_rows[:, part, :], op=ALU.add).then_inc(pool_step, 1)
                pool.wait_ge(pool_step, n + 1)
                nc.gpsimd.tensor_tensor(out=fm_sq[:, part, :], in0=fm_total[:, part, :],
                                        in1=fm_total[:, part, :], op=ALU.mult).then_inc(sum_sq_done, 1)

        @block.scalar
        def _(act):
            def scale_split(g, parity):
                nc.scalar.activation(r(sc_hi[:, parity, :]), scale_b[:, cols(g)], ACT.Copy)
                nc.scalar.mul(sc_raw[:, parity, :], scale_b[:, cols(g)],
                              consts[0:ROWS_X, 2:3]).then_inc(scale_parts, 1)

            def pad_copy(g, parity):
                act.wait_ge(user_in[parity], pad_level(g, parity))
                nc.scalar.activation(user_pad[:, parity, :, EMB:P], user_rows[:, tiles(g), :],
                                     ACT.Copy).then_inc(pad_ready, 1)

            def pad_level(g, parity):
                return (g - parity) * (16 * TILES_PER_GROUP // 2) + 16 * TILES_PER_GROUP

            act.wait_ge(early_in, 16)
            nc.scalar.activation(fold_t[EMB:P, 0, :], fold_t[EMB:P, 0, :], ACT.Tanh)
            nc.scalar.activation(fold_t[:, 1, :], fold_t[:, 1, :], ACT.Tanh).then_inc(tables_tanh, 1)
            act.wait_ge(first_in, 16)
            scale_split(0, 0)
            act.wait_ge(fold_done, 1)
            nc.scalar.activation(r(fold_hi[:]), ps_l2[0][0:ROWS_X, :], ACT.Copy).then_inc(fold_hi_done, 1)
            act.wait_ge(pad_zeroed, 1)
            pad_copy(0, 0)
            act.wait_ge(w1_in, 16)
            nc.scalar.activation(r(w1_hi[:]), w1_raw[:], ACT.Copy).then_inc(w1_hi_done, 1)

            def w2_split(k):
                nc.scalar.activation(r(w2_hi[:, k, :]), w2_raw[:, k, :], ACT.Copy).then_inc(w2_hi_done, 1)

            act.wait_ge(second_in, 16)
            scale_split(1, 1)
            act.wait_ge(late_in, 16)
            act.wait_ge(xa_ready, 1)
            nc.scalar.activation(r(xa_hi[:, 0, :]), ps_xa[:, 0:GROUP], ACT.Identity,
                                 bias=visb[:, 0:1]).then_inc(xa_hi_done, 1)
            act.wait_ge(w2_in[0], 16)
            w2_split(0)
            w2_split(1)
            act.wait_ge(w2_in[1], 16)
            w2_split(2)
            pad_copy(1, 1)
            w2_split(3)

            def hidden_hi(g, parity):
                for j in range(2):
                    act.wait_ge(h_ready, g * 2 + j + 1)
                    nc.scalar.activation(r(h_hi[:, parity, 2 * j:2 * j + 2, :]), ps_h[j][:],
                                         ACT.Relu).then_inc(h_hi_done, 1)

            hidden_hi(0, 0)
            act.wait_ge(tab_in, 16)
            nc.scalar.activation(tab[:, EMB:2 * EMB], tab[:, EMB:2 * EMB], ACT.Tanh).then_inc(act_step, 1)
            act.wait_ge(act_step, 1)
            nc.scalar.activation(norm_sink[:, 0, :], tab[:, 0:EMB], ACT.Square,
                                 accum_out=tab[:, 2 * EMB + 2:2 * EMB + 3])
            nc.scalar.activation(norm_sink[:, 1, :], tab[:, EMB:2 * EMB], ACT.Square,
                                 accum_out=tab[:, 2 * EMB + 3:2 * EMB + 4]).then_inc(act_step, 1)
            act.wait_ge(act_step, 2)
            nc.scalar.activation(r(tab_hi[:]), tab[:], ACT.Copy).then_inc(tab_hi_done, 1)

            def step(g, parity, codes_ahead):
                nxt = 1 - parity
                act.wait_ge(xa_ready, g + 2)
                nc.scalar.activation(r(xa_hi[:, nxt, :]), ps_xa[:, 0:GROUP], ACT.Identity,
                                     bias=visb[:, 0:1]).then_inc(xa_hi_done, 1)
                if codes_ahead:
                    pad_copy(g + 2, parity)
                    act.wait_ge(rest_in, (g - parity) * 8 + 16)
                    act.wait_ge(scale_merged, g + 1)
                    scale_split(g + 2, parity)
                hidden_hi(g + 1, nxt)

            with act.Fori(0, LOOP_STEPS // 2) as i:
                for parity in range(2):
                    step(i * 2 + parity, parity, True)
            step(GROUPS - 2, 0, False)
            act.wait_ge(logits_shifted, 1)
            nc.scalar.activation(expd[:], shifted[:], ACT.Exp).then_inc(exp_done, 1)

        @block.vector
        def _(dve):
            linked = [0]

            def link(ins):
                linked[0] += 1
                ins.then_inc(dve_step, 1)
                dve.wait_ge(dve_step, linked[0])

            nc.vector.memset(warm[:], 0.0).then_inc(warm_zeroed, 1)
            dve.wait_ge(ids_in, 16)
            for n, (size, idx, ready) in enumerate(((USERS, emb_idx, emb_idx_ready), (VOCAB, fm_idx, fm_idx_ready))):
                link(nc.vector.tensor_scalar(id_neg[:, n, :], ids[:], 0.0, float(size), ALU.is_lt, ALU.mult))
                link(nc.vector.tensor_tensor(id_wrap[:, n, :], id_neg[:, n, :], ids[:], ALU.add))
                nc.vector.tensor_scalar(idx[:], id_wrap[:, n, :], 0.0, float(size - 1), ALU.max,
                                        ALU.min).then_inc(ready, 1)
            nc.vector.memset(inv[:], 0.0).then_inc(l2_free, 4)
            nc.vector.memset(denom[:], 0.0).then_inc(dots_done, 4)
            nc.vector.memset(top[:], 0.0).then_inc(fm_taken, 1)

            def make_hots(g, parity):
                dve.wait_ge(scale_parts, g + 1)
                nc.vector.scalar_tensor_tensor(out=sc_part[:, parity, :], in0=sc_hi[:, parity, :],
                                               scalar=consts[0:ROWS_X, 1:2], in1=sc_raw[:, parity, :],
                                               op0=ALU.mult, op1=ALU.add).then_inc(scale_merged, 1)
                nc.vector.tensor_scalar(r(hot[:, parity, :]), codes[0:ROWS_A, cols(g)],
                                        consts[0:ROWS_A, 0:1], None, ALU.is_equal)
                dve.wait_ge(scale_merged, g + 1)
                nc.vector.scalar_tensor_tensor(out=r(hot_scaled[:, parity, :]), in0=codes[:, cols(g)],
                                               scalar=consts[0:ROWS_X, 0:1], in1=sc_part[:, parity, :],
                                               op0=ALU.is_equal, op1=ALU.mult).then_inc(hots_ready, 1)

            def inputs_lo(g, parity):
                dve.wait_ge(xa_hi_done, g + 1)
                nc.vector.scalar_tensor_tensor(out=r(xa_lo[:, parity, :]), in0=ps_xa[:, 0:GROUP],
                                               scalar=visb[:, 0:1], in1=xa_hi[:, parity, :],
                                               op0=ALU.add, op1=ALU.subtract).then_inc(xa_lo_done, 1)

            def hidden_lo(g, parity):
                for j in range(2):
                    dve.wait_ge(h_hi_done, g * 2 + j + 1)
                    nc.vector.scalar_tensor_tensor(out=r(h_lo[:, parity, 2 * j:2 * j + 2, :]), in0=ps_h[j][:],
                                                   scalar=0.0, in1=h_hi[:, parity, 2 * j:2 * j + 2, :],
                                                   op0=ALU.max, op1=ALU.subtract).then_inc(h_lo_done, 1)

            def fm_take(g, parity):
                dve.wait_ge(fm_ready, g + 1)
                ps = ps_fm[:, 0:TILES_PER_GROUP * FM_COLS].rearrange("p (t c) -> p t c", c=FM_COLS)
                nc.vector.tensor_copy(fm_small[:, tiles(g), :], ps[:, :, 2 * EMB:FM_COLS])
                for t in range(TILES_PER_GROUP):
                    last = nc.vector.tensor_scalar(face_scaled[:, parity, t, :], ps[:, t, EMB:2 * EMB],
                                                   scale_c[:, bass.ds(g * TILES_PER_GROUP + t, 1)], None, ALU.mult)
                last.then_inc(fm_face_done, 1)
                dve.wait_ge(fm_face_done, g + 1)
                nc.vector.tensor_tensor(out=fm_sum[:, tiles(g), :], in0=ps[:, :, 0:EMB],
                                        in1=face_scaled[:, parity, :, :], op=ALU.add).then_inc(fm_taken, 1)

            def output_dots(g, parity, t):
                slot = 2 * parity + t
                dve.wait_ge(l2_ready, g * 2 + t + 1)
                dve.wait_ge(dots_done, g * 2 + t + 1)
                nc.vector.tensor_tensor(out=hidden2[:, slot, :], in0=ps_l2[slot][:], in1=b2_b,
                                        op=ALU.add).then_inc(l2_free, 1)
                dve.wait_ge(l2_free, g * 2 + t + 5)
                for j in range(2):
                    last = nc.vector.scalar_tensor_tensor(
                        out=dot_sink[:, slot, j, :], in0=hidden2[:, slot, :], scalar=0.0, in1=w3_b[:, j, :],
                        op0=ALU.max, op1=ALU.mult, accum_out=mlp[:, bass.ds(g * 2 + t, 1), j])
                last.then_inc(dots_done, 1)

            dve.wait_ge(first_in, 16)
            make_hots(0, 0)
            dve.wait_ge(fold_hi_done, 1)
            nc.vector.tensor_tensor(r(fold_lo[:]), ps_l2[0][0:ROWS_X, :], fold_hi[:],
                                    ALU.subtract).then_inc(fold_lo_done, 1)
            dve.wait_ge(w1_hi_done, 1)
            nc.vector.tensor_tensor(r(w1_lo[:]), w1_raw[:], w1_hi[:], ALU.subtract).then_inc(w1_lo_done, 1)

            def w2_rest(k):
                dve.wait_ge(w2_hi_done, k + 1)
                nc.vector.tensor_tensor(r(w2_lo[:, k, :]), w2_raw[:, k, :], w2_hi[:, k, :],
                                        ALU.subtract).then_inc(w2_lo_done, 1)

            inputs_lo(0, 0)
            for k in range(KT):
                w2_rest(k)
            hidden_lo(0, 0)
            dve.wait_ge(second_in, 16)
            make_hots(1, 1)
            dve.wait_ge(tab_hi_done, 1)
            nc.vector.tensor_tensor(r(tab_lo[:]), tab[:], tab_hi[:], ALU.subtract).then_inc(tab_lo_done, 1)
            dve.wait_ge(scale_c_in, 16)
            dve.wait_ge(out_rows_in, 16)

            def step(g, parity):
                nxt = 1 - parity
                inputs_lo(g + 1, nxt)
                output_dots(g, parity, 0)
                fm_take(g, parity)
                dve.wait_ge(rest_in, (g - parity) * 8 + 16)
                make_hots(g + 2, parity)
                hidden_lo(g + 1, nxt)
                output_dots(g, parity, 1)

            with dve.Fori(0, LOOP_STEPS // 2) as i:
                for parity in range(2):
                    step(i * 2 + parity, parity)
            inputs_lo(GROUPS - 1, 1)
            fm_take(GROUPS - 2, 0)
            dve.wait_ge(user_norm_done, 1)
            nc.vector.reduce_sum(user_norm[:], user_sq[:], axis=AX)
            nc.vector.tensor_tensor(scale2[:], scale_c[:], scale_c[:], ALU.mult)
            output_dots(GROUPS - 2, 0, 0)
            fm_take(GROUPS - 1, 1)
            hidden_lo(GROUPS - 1, 1)
            dve.wait_ge(fm_rows_in, 16 * TILES)
            dve.wait_ge(fm_taken, GROUPS + 1)
            nc.vector.tensor_tensor(base_lin[:], fm_small[:, :, 0:2], fm_rows[:], ALU.add)
            nc.vector.tensor_tensor(norms[:, 0, :], user_norm[:], fm_small[:, :, 2], ALU.add)
            link(nc.vector.tensor_tensor(norms[:, 1, :], scale2[:], fm_small[:, :, 3], ALU.mult))
            nc.vector.tensor_tensor(norms[:, 2, :], norms[:, 0, :], norms[:, 1, :], ALU.add)
            dve.wait_ge(sum_sq_done, 2)
            link(nc.vector.reduce_sum(sum_sq[:], fm_sq[:], axis=AX))
            output_dots(GROUPS - 2, 0, 1)
            link(nc.vector.tensor_tensor(norms[:, 3, :], sum_sq[:], norms[:, 2, :], ALU.subtract))
            for j in range(2):
                last = nc.vector.scalar_tensor_tensor(out=base[:, :, j], in0=norms[:, 3, :], scalar=0.5,
                                                      in1=base_lin[:, :, j], op0=ALU.mult, op1=ALU.add)
            link(last)
            output_dots(GROUPS - 1, 1, 0)
            output_dots(GROUPS - 1, 1, 1)

            dve.wait_ge(dots_done, 4 + TILES)
            link(nc.vector.tensor_tensor(logits[:], mlp[:], base[:], ALU.add))
            link(nc.vector.tensor_tensor(top[:], logits[:, :, 0], logits[:, :, 1], ALU.max))
            both = lambda x: x[:].rearrange("p (t a) -> p t a", a=1).to_broadcast([P, TILES, 2])
            nc.vector.tensor_tensor(shifted[:], logits[:], both(top), ALU.subtract).then_inc(logits_shifted, 1)
            dve.wait_ge(exp_done, 1)
            link(nc.vector.tensor_tensor(denom[:], expd[:, :, 0], expd[:, :, 1], ALU.add))
            link(nc.vector.reciprocal(inv[:], denom[:]))
            nc.vector.tensor_tensor(probs[:], expd[:], both(inv), ALU.mult).then_inc(probs_done, 1)

        @block.tensor
        def _(pe):
            def front(g, parity):
                pe.wait_ge(pad_ready, g + 1)
                for t in range(TILES_PER_GROUP):
                    nc.tensor.transpose(ps_xa[:, t * P:(t + 1) * P], user_pad[:, parity, t, :], ident[:])
                for k in range(2):
                    last = nc.tensor.matmul(ps_xa[0:EMB, 0:GROUP], visw[:, k, :], vis_in[:, k, cols(g)],
                                            start=(k == 0), stop=(k == 1))
                last.then_inc(xa_ready, 1)

            def layer1_tables(m, parity, start=True):
                o = ps_h[m // 2][:, m % 2, :]
                mc = slice(m * P, (m + 1) * P)
                nc.tensor.matmul(o, r(fold_hi[:, mc]), r(hot_scaled[:, parity, :]), start=start, stop=False)
                nc.tensor.matmul(o, r(fold_lo[0:ROWS_A, mc]), r(hot_scaled[0:ROWS_A, parity, :]),
                                 start=False, stop=False)

            def layer1_hi(m, parity):
                o = ps_h[m // 2][:, m % 2, :]
                mc = slice(m * P, (m + 1) * P)
                nc.tensor.matmul(o, r(w1_hi[:, mc]), r(xa_hi[:, parity, :]), start=False, stop=False)
                nc.tensor.matmul(o, r(w1_lo[:, mc]), r(xa_hi[:, parity, :]), start=False, stop=False)

            def layer1_lo(m, parity, stop=True):
                last = nc.tensor.matmul(ps_h[m // 2][:, m % 2, :], r(w1_hi[:, m * P:(m + 1) * P]),
                                        r(xa_lo[:, parity, :]), start=False, stop=stop)
                if m % 2 == 1:
                    last.then_inc(h_ready, 1)

            def layer1(g, parity):
                pe.wait_ge(hots_ready, g + 1)
                pe.wait_ge(xa_lo_done, g + 1)
                for m in range(KT):
                    layer1_tables(m, parity)
                    layer1_hi(m, parity)
                    layer1_lo(m, parity)

            def lookups(g, parity):
                pe.wait_ge(tab_lo_done, 1)
                pe.wait_ge(hots_ready, g + 1)
                pe.wait_ge(fm_taken, g + 1)
                for t in range(TILES_PER_GROUP):
                    o = ps_fm[:, t * FM_COLS:(t + 1) * FM_COLS]
                    h = r(hot[:, parity, t * P:(t + 1) * P])
                    nc.tensor.matmul(o, h, r(tab_hi[:]), start=True, stop=False)
                    last = nc.tensor.matmul(o, h, r(tab_lo[:]), start=False, stop=True)
                last.then_inc(fm_ready, 1)

            def layer2(g, parity, t):
                pe.wait_ge(l2_free, g * 2 + t + 1)
                o = ps_l2[2 * parity + t][:]
                tc = slice(t * P, (t + 1) * P)
                for k in range(KT):
                    if t == 0 and k % 2 == 0:
                        pe.wait_ge(h_lo_done, g * 2 + k // 2 + 1)
                    hi = r(h_hi[:, parity, k, tc])
                    lo = r(h_lo[:, parity, k, tc])
                    nc.tensor.matmul(o, hi, r(w2_hi[:, k, :]), start=(k == 0), stop=False)
                    nc.tensor.matmul(o, hi, r(w2_lo[:, k, :]), start=False, stop=False)
                    last = nc.tensor.matmul(o, lo, r(w2_hi[:, k, :]), start=False, stop=(k == KT - 1))
                last.then_inc(l2_ready, 1)

            def keep_warm(count):
                for _ in range(count):
                    nc.tensor.matmul(ps_l2[3][:], warm[:, 0:P], warm[:], start=True, stop=True)

            pe.wait_ge(warm_zeroed, 1)
            keep_warm(WARM_UP[0])
            pe.wait_ge(tables_tanh, 1)
            pe.wait_ge(fold_in, 16)
            o = ps_l2[0][0:ROWS_X, :]
            for n in range(2):
                nc.tensor.matmul(o, fold_t[:, n, :], fold_w_sb[:, n, :], start=(n == 0), stop=False)
            pe.wait_ge(b1_in, 16)
            nc.tensor.matmul(o, b1_sb[:, HIDDEN:HIDDEN + ROWS_X], b1_sb[:, 0:HIDDEN], start=False,
                             stop=True).then_inc(fold_done, 1)
            keep_warm(WARM_UP[1])
            pe.wait_ge(late_in, 16)
            pe.wait_ge(vis_first_in, 16)
            front(0, 0)
            pe.wait_ge(fold_lo_done, 1)
            pe.wait_ge(hots_ready, 1)
            for m in range(KT):
                layer1_tables(m, 0, start=(m % 2 == 0))
            pe.wait_ge(w1_lo_done, 1)
            pe.wait_ge(xa_hi_done, 1)
            for m in range(KT):
                layer1_hi(m, 0)
            pe.wait_ge(xa_lo_done, 1)
            for m in range(KT):
                layer1_lo(m, 0, stop=(m % 2 == 1))
            keep_warm(WARM_UP[2])
            pe.wait_ge(vis_second_in, 16)
            front(1, 1)

            def step(g, parity):
                layer2(g, parity, 0)
                lookups(g, parity)
                layer1(g + 1, 1 - parity)
                layer2(g, parity, 1)
                if parity == 0:
                    pe.wait_ge(vis_rest_in, g * 8 + 16)
                front(g + 2, parity)

            pe.wait_ge(w2_lo_done, KT)
            with pe.Fori(0, LOOP_STEPS // 2) as i:
                for parity in range(2):
                    step(i * 2 + parity, parity)
            lookups(GROUPS - 2, 0)
            layer2(GROUPS - 2, 0, 0)
            lookups(GROUPS - 1, 1)
            layer1(GROUPS - 1, 1)
            layer2(GROUPS - 2, 0, 1)
            layer2(GROUPS - 1, 1, 0)
            layer2(GROUPS - 1, 1, 1)


def kernel(r_visual, r_user_id, r_hour, r_scale, r_gender, r_age, r_attribute, L0_rec_user_emb,
           L0_rec_hour_emb, L0_rec_gender_emb, L0_rec_age_emb, L0_rec_attr_emb, L0_rec_visu_w,
           L0_rec_visu_b, L0_rec_fm_w, L0_rec_fm_b, L0_rec_w1, L0_rec_b1, L0_rec_w2, L0_rec_b2,
           L0_rec_w3, L0_rec_b3):
    import numpy as np
    import concourse.bacc as bacc
    from concourse.bass_utils import run_bass_kernel_spmd

    f32 = np.float32
    visual = np.asarray(r_visual).T.reshape(2, P, ROWS).transpose(1, 0, 2)
    by_tile = lambda a: np.asarray(a).reshape(TILES, P).T

    ids = [np.asarray(a)[None, :] for a in (r_hour, r_gender, r_age, r_attribute)]
    repeated = [np.repeat(a, n, axis=0) for a, n in zip(ids, FIELD_SIZES)]
    code_rows = np.concatenate(repeated + [np.zeros((BIAS_ROWS, ROWS), ids[0].dtype)] + repeated[1:])
    scale = np.asarray(r_scale).reshape(1, ROWS)
    scale_rows = np.concatenate([np.ones((FIELD_SIZES[0], ROWS), f32), np.repeat(scale, ROWS_B, axis=0),
                                 np.ones((BIAS_ROWS, ROWS), f32), np.repeat(scale, ROWS_B, axis=0)])
    lookup_inputs = np.stack([code_rows, scale_rows.view(np.int32)], axis=1)

    numbers = [np.arange(n) for n in FIELD_SIZES]
    consts = np.zeros((P, CONST_COLS), f32)
    consts[0:ROWS_X, 0] = np.concatenate(numbers + [np.zeros(BIAS_ROWS)] + numbers[1:])
    consts[0:ROWS_A, 1] = 1.0
    consts[ROWS_A:ROWS_X, 1] = -1.0
    consts[ROWS_A:ROWS_X, 2] = 1.0

    w1t = np.asarray(L0_rec_w1).T
    user_w, hour_w, gender_w, attr_w, age_w, vis_w = (w1t[n * EMB:(n + 1) * EMB] for n in range(6))
    fold_w = np.stack([np.concatenate([hour_w, age_w]), np.concatenate([gender_w, attr_w])], axis=1)
    hour, gender, age, attr = (np.asarray(a) for a in (L0_rec_hour_emb, L0_rec_gender_emb,
                                                       L0_rec_age_emb, L0_rec_attr_emb))
    starts = np.cumsum((0,) + FIELD_SIZES)
    fold_tables = np.zeros((P, 2, ROWS_X), f32)
    lookup_tables = np.zeros((ROWS_A, 2 * EMB + 2), f32)
    for n, (table, top, pair) in enumerate(((hour, 0, 0), (gender, 0, 1), (age, EMB, 0), (attr, EMB, 1))):
        at = starts[n]
        fold_tables[top:top + EMB, pair, at:at + len(table)] = table.T
        lookup_tables[at:at + len(table), min(n, 1) * EMB:(min(n, 1) + 1) * EMB] = table
        if n:
            at += ROWS_A - FIELD_SIZES[0]
            fold_tables[top:top + EMB, pair, at:at + len(table)] = table.T
    fm_rows = np.asarray(L0_rec_fm_w).T
    lookup_tables[0:LOOKUP, 2 * EMB:] = fm_rows[USERS:]
    lookup_tables[LOOKUP, 2 * EMB:] = L0_rec_fm_b
    lookup_tables[LOOKUP + 1, 2 * EMB:] = L0_rec_b3
    b1_row = np.zeros((1, HIDDEN + ROWS_X), f32)
    b1_row[0, 0:HIDDEN] = L0_rec_b1
    b1_row[0, HIDDEN + LOOKUP] = 1.0
    visu_w = np.asarray(L0_rec_visu_w).T.reshape(2, P, EMB).transpose(1, 0, 2)
    visu_b = np.concatenate([np.asarray(L0_rec_visu_b), np.zeros(EMB, f32)])[:, None]

    arrays = {
        "visual": visual,
        "user_ids": by_tile(r_user_id),
        "lookup_inputs": lookup_inputs,
        "scale_cols": by_tile(r_scale),
        "user_emb": L0_rec_user_emb,
        "fm_user": fm_rows,
        "hidden1_w": np.concatenate([vis_w, user_w]),
        "fold_w": fold_w,
        "small_early": np.concatenate([fold_tables.reshape(P, -1), consts], axis=1),
        "small_late": np.concatenate([visu_w.reshape(P, -1), visu_b, np.eye(P, dtype=f32)], axis=1),
        "b1_row": b1_row,
        "lookup_tables": lookup_tables,
        "w2": np.asarray(L0_rec_w2).T.reshape(KT, P, HIDDEN).transpose(1, 0, 2),
        "out_rows": np.concatenate([np.asarray(L0_rec_b2)[None, :], L0_rec_w3]),
    }
    arrays = {name: np.ascontiguousarray(a) for name, a in arrays.items()}
    nc = bacc.Bacc("TRN2", target_bir_lowering=False, num_devices=1)
    aps = [nc.dram_tensor(name, a.shape, mybir.dt.from_np(a.dtype), kind="ExternalInput").ap()
           for name, a in arrays.items()]
    out = nc.dram_tensor("out", (P, TILES, 2), mybir.dt.float32, kind="ExternalOutput").ap()
    rec_program(nc, *aps, out)
    result = run_bass_kernel_spmd(nc, [arrays], core_ids=[0])
    return result.results[0]["out"].transpose(1, 0, 2).reshape(ROWS, 2)
```

```python
import concourse.bass as bass
from concourse import mybir
from contextlib import ExitStack

P = 128
ROWS = 2048
GROUP = 256
TILES_PER_GROUP = GROUP // P
GROUPS = ROWS // GROUP
TILES = ROWS // P
EMB = 64
VIS = 256
HIDDEN = 512
HALF = HIDDEN // 2
KT = HIDDEN // P
FIELD_SIZES = (24, 2, 8, 40)
LOOKUP = sum(FIELD_SIZES)
BIAS_ROWS = 2
ROWS_A = LOOKUP + BIAS_ROWS
ROWS_B = LOOKUP - FIELD_SIZES[0]
ROWS_X = ROWS_A + ROWS_B
USERS = 125000
VOCAB = USERS + LOOKUP
WARM_UP = (10, 5, 3)
FM_COLS = 2 * EMB + 4


FOLD_COLS = 2 * ROWS_X
CONST_COLS = 3
VISW_COLS = 2 * P
SMALL_EARLY = FOLD_COLS + CONST_COLS
SMALL_LATE = VISW_COLS + 1 + P


def rec_program(nc, visual, user_ids, lookup_inputs, scale_cols, user_emb, fm_user, hidden1_w, fold_w,
                small_early, small_late, b1_row, lookup_tables, w2, out_rows, out):
    fp32 = mybir.dt.float32
    fp32r = mybir.dt.float32r
    i32 = mybir.dt.int32
    ALU = mybir.AluOpType
    ACT = mybir.ActivationFunctionType
    AX = mybir.AxisListType.X

    ctx = ExitStack()
    with ctx:
        def sb(name, shape, dt=fp32):
            return ctx.enter_context(nc.sbuf_tensor(name, shape, dt))

        def pb(name, shape, dt=fp32):
            return ctx.enter_context(nc.psum_tensor(name, shape, dt))

        def sem(name):
            return ctx.enter_context(nc.semaphore(name))

        def r(ap):
            return ap.bitcast(fp32r)

        ids = sb("ids", [P, TILES], i32)
        lookup_in = sb("lookup_in", [ROWS_X, 2, ROWS], i32)
        codes = lookup_in[:, 0, :]
        scale_b = lookup_in[:, 1, :].bitcast(fp32)
        scale_c = sb("scale_c", [P, TILES])
        vis_in = sb("vis_in", [P, 2, ROWS])
        early = sb("early", [P, SMALL_EARLY])
        late = sb("late", [P, SMALL_LATE])
        fold_t = early[:, 0:FOLD_COLS].rearrange("p (n r) -> p n r", n=2)
        consts = early[:, FOLD_COLS:SMALL_EARLY]
        visw = late[:, 0:VISW_COLS].rearrange("p (k d) -> p k d", k=2)
        visb = late[:, VISW_COLS:VISW_COLS + 1]
        ident = late[:, VISW_COLS + 1:SMALL_LATE]
        b1_sb = sb("b1_sb", [1, HIDDEN + ROWS_X])
        w1_raw = sb("w1_raw", [P, HIDDEN])
        fold_w_sb = sb("fold_w_sb", [P, 2, HIDDEN])
        tab = sb("tab", [ROWS_A, FM_COLS])
        w2_raw = sb("w2_raw", [P, KT, HIDDEN])
        out_b = sb("out_b", [P, 3, HIDDEN])
        b2_b = out_b[:, 0, :]
        w3_b = out_b[:, 1:3, :]
        warm = sb("warm", [P, HIDDEN], mybir.dt.bfloat16)
        visw_hi = sb("visw_hi", [P, 2, P])
        visw_lo = sb("visw_lo", [P, 2, P])
        w1_hi = sb("w1_hi", [P, HIDDEN])
        w1_lo = sb("w1_lo", [P, HIDDEN])
        w2_hi = sb("w2_hi", [P, KT, HIDDEN])
        w2_lo = sb("w2_lo", [P, KT, HIDDEN])
        fold_hi = sb("fold_hi", [ROWS_X, HIDDEN])
        fold_lo = sb("fold_lo", [ROWS_X, HIDDEN])
        norm_sink = sb("norm_sink", [ROWS_A, 2, EMB])
        tab_hi = sb("tab_hi", [ROWS_A, FM_COLS])
        tab_lo = sb("tab_lo", [ROWS_A, FM_COLS])
        id_neg = sb("id_neg", [P, 2, TILES])
        id_wrap = sb("id_wrap", [P, 2, TILES])
        emb_idx = sb("emb_idx", [P, TILES], i32)
        fm_idx = sb("fm_idx", [P, TILES], i32)
        user_rows = sb("user_rows", [P, TILES, EMB])
        fm_rows = sb("fm_rows", [P, TILES, 2])
        user_pad = sb("user_pad", [P, 2, TILES_PER_GROUP, P])
        sc_hi = sb("sc_hi", [ROWS_X, 2, GROUP])
        sc_raw = sb("sc_raw", [ROWS_X, 2, GROUP])
        sc_part = sb("sc_part", [ROWS_X, 2, GROUP])
        hot_scaled = sb("hot_scaled", [ROWS_X, 2, GROUP])
        hot = sb("hot", [ROWS_A, 2, GROUP])
        vis_hi = sb("vis_hi", [P, 2, 2, GROUP])
        vis_lo = sb("vis_lo", [P, 2, 2, GROUP])
        xa_hi = sb("xa_hi", [P, 2, GROUP])
        xa_lo = sb("xa_lo", [P, 2, GROUP])
        h_hi = sb("h_hi", [P, 2, KT, GROUP])
        h_lo = sb("h_lo", [P, 2, KT, GROUP])
        face_scaled = sb("face_scaled", [P, 2, TILES_PER_GROUP, EMB])
        fm_sum = sb("fm_sum", [P, TILES, EMB])
        fm_small = sb("fm_small", [P, TILES, 4])
        fm_total = sb("fm_total", [P, TILES, EMB])
        fm_sq = sb("fm_sq", [P, TILES, EMB])
        square_sink = sb("square_sink", [P, 4, EMB])
        tail_dots = sb("tail_dots", [P, 2, 2])
        sum_sq = sb("sum_sq", [P, TILES])
        user_norm = sb("user_norm", [P, TILES])
        scale2 = sb("scale2", [P, TILES])
        norms = sb("norms", [P, 4, TILES])
        base_lin = sb("base_lin", [P, TILES, 2])
        base = sb("base", [P, TILES, 2])
        hidden2 = sb("hidden2", [P, 4, HIDDEN])
        dot_sink = sb("dot_sink", [P, 4, 2, HIDDEN])
        mlp = sb("mlp", [P, TILES, 2])
        logits = sb("logits", [P, TILES, 2])
        top = sb("top", [P, TILES])
        shifted = sb("shifted", [P, TILES, 2])
        expd = sb("expd", [P, TILES, 2])
        denom = sb("denom", [P, TILES])
        inv = sb("inv", [P, TILES])
        probs = sb("probs", [P, TILES, 2])

        ps_xa = pb("ps_xa", [P, 512])
        ps_h = [pb(f"ps_h{j}", [P, 2, GROUP]) for j in range(2)]
        ps_fm = pb("ps_fm", [P, 512])
        ps_l2 = [pb(f"ps_l2_{j}", [P, HIDDEN]) for j in range(4)]

        ids_in = sem("ids_in")
        first_in = sem("first_in")
        second_in = sem("second_in")
        rest_in = sem("rest_in")
        vis_first_in = sem("vis_first_in")
        vis_second_in = sem("vis_second_in")
        vis_rest_in = sem("vis_rest_in")
        early_in = sem("early_in")
        late_in = sem("late_in")
        w1_in = sem("w1_in")
        fold_in = sem("fold_in")
        tab_in = sem("tab_in")
        w2_in = [sem(f"w2_in{k}") for k in range(2)]
        out_rows_in = sem("out_rows_in")
        b1_in = sem("b1_in")
        scale_c_in = sem("scale_c_in")
        user_in = [sem(f"user_in{p}") for p in range(2)]
        fm_rows_in = sem("fm_rows_in")
        out_done = sem("out_done")
        dve_step = sem("dve_step")
        act_step = sem("act_step")
        pad_zeroed = sem("pad_zeroed")
        emb_idx_ready = sem("emb_idx_ready")
        fm_idx_ready = sem("fm_idx_ready")
        tables_tanh = sem("tables_tanh")
        fold_done = sem("fold_done")
        fold_hi_done = sem("fold_hi_done")
        fold_lo_done = sem("fold_lo_done")
        w1_hi_done = sem("w1_hi_done")
        w1_lo_done = sem("w1_lo_done")
        w2_hi_done = sem("w2_hi_done")
        w2_lo_done = sem("w2_lo_done")
        w2_first_lo_done = sem("w2_first_lo_done")
        tab_hi_done = sem("tab_hi_done")
        tab_lo_done = sem("tab_lo_done")
        warm_zeroed = sem("warm_zeroed")
        dots_done = sem("dots_done")
        pad_ready = sem("pad_ready")
        scale_parts = sem("scale_parts")
        scale_merged = sem("scale_merged")
        hots_ready = sem("hots_ready")
        visw_hi_done = sem("visw_hi_done")
        visw_lo_done = sem("visw_lo_done")
        vis_hi_done = sem("vis_hi_done")
        vis_lo_done = sem("vis_lo_done")
        xa_ready = sem("xa_ready")
        xa_hi_done = sem("xa_hi_done")
        xa_lo_done = sem("xa_lo_done")
        h_ready = sem("h_ready")
        h_hi_done = sem("h_hi_done")
        h_lo_done = sem("h_lo_done")
        fm_ready = sem("fm_ready")
        fm_face_done = sem("fm_face_done")
        fm_taken = sem("fm_taken")
        l2_ready = sem("l2_ready")
        l2_free = sem("l2_free")
        user_norm_done = sem("user_norm_done")
        totals_ready = sem("totals_ready")
        squares_ready = sem("squares_ready")
        sum_sq_done = sem("sum_sq_done")
        halves_done = sem("halves_done")
        base_done = sem("base_done")
        logits_shifted = sem("logits_shifted")
        exp_done = sem("exp_done")
        probs_done = sem("probs_done")

        LOOP_STEPS = GROUPS - 2
        TAIL = LOOP_STEPS * TILES_PER_GROUP

        def cols(g):
            return bass.ds(g * GROUP, GROUP)

        def tiles(g):
            return bass.ds(g * TILES_PER_GROUP, TILES_PER_GROUP)

        projected = ps_xa[0:EMB, 0:GROUP]
        transposed = ps_xa[EMB:P, GROUP:2 * GROUP]

        def tail_bank(n):
            return ps_l2[(2, 1, 3, 0)[n]]

        block = ctx.enter_context(nc.Block())

        @block.sync
        def _(sp):
            def rows(lo, hi, arrived, vis_arrived):
                sp.dma_start(lookup_in[:, :, lo:hi], lookup_inputs[:, :, lo:hi]).then_inc(arrived, 16)
                sp.dma_start(vis_in[:, :, lo:hi], visual[:, :, lo:hi]).then_inc(vis_arrived, 16)

            sp.dma_start(ids[:], user_ids).then_inc(ids_in, 16)
            sp.dma_start(early[:], small_early).then_inc(early_in, 16)
            sp.dma_start(fold_w_sb[:], fold_w).then_inc(fold_in, 16)
            sp.dma_start(b1_sb[:], b1_row).then_inc(b1_in, 16)
            sp.dma_start(late[:], small_late).then_inc(late_in, 16)
            sp.dma_start(tab[:, 0:2 * EMB + 2], lookup_tables).then_inc(tab_in, 16)
            rows(0, GROUP, first_in, vis_first_in)
            sp.dma_start(w1_raw[:], hidden1_w).then_inc(w1_in, 16)
            rows(GROUP, 2 * GROUP, second_in, vis_second_in)
            for k in range(2):
                sp.dma_start(w2_raw[:, 2 * k:2 * k + 2, :], w2[:, 2 * k:2 * k + 2, :]).then_inc(w2_in[k], 16)
            sp.dma_start(scale_c[:], scale_cols).then_inc(scale_c_in, 16)
            sp.dma_start(out_b[:], out_rows.rearrange("(a j) n -> a j n", a=1)
                         .to_broadcast([P, 3, HIDDEN])).then_inc(out_rows_in, 16)
            for pair in range(1, GROUPS // 2):
                if pair > 1:
                    sp.wait_ge(rest_in, 16 * (pair - 1))
                    sp.wait_ge(vis_rest_in, 16 * (pair - 1))
                rows(pair * 2 * GROUP, (pair + 1) * 2 * GROUP, rest_in, vis_rest_in)
            sp.wait_ge(probs_done, 1)
            sp.dma_start(out, probs[:]).then_inc(out_done, 16)
            sp.wait_ge(out_done, 16)

        @block.gpsimd
        def _(pool):
            nc.gpsimd.memset(user_pad[:], 0.0).then_inc(pad_zeroed, 1)
            pool.wait_ge(emb_idx_ready, 1)
            for t in range(TILES):
                g = t // TILES_PER_GROUP
                if t == 3 * TILES_PER_GROUP:
                    pool.wait_ge(w2_hi_done, 1)
                    nc.gpsimd.tensor_tensor(out=r(w2_lo[:, 0, :]), in0=w2_raw[:, 0, :],
                                            in1=w2_hi[:, 0, :], op=ALU.subtract).then_inc(w2_first_lo_done, 1)
                if t % TILES_PER_GROUP == 0 and g >= 2:
                    pool.wait_ge(user_in[g % 2], 16 * TILES_PER_GROUP * (g // 2))
                nc.gpsimd.indirect_dma_start(
                    out=user_rows[:, t, :], out_offset=None, in_=user_emb,
                    in_offset=bass.IndirectOffsetOnAxis(ap=emb_idx[:, t:t + 1], axis=0),
                ).then_inc(user_in[g % 2], 16)
            pool.wait_ge(fm_idx_ready, 1)
            for t in range(TILES):
                nc.gpsimd.indirect_dma_start(
                    out=fm_rows[:, t, :], out_offset=None, in_=fm_user,
                    in_offset=bass.IndirectOffsetOnAxis(ap=fm_idx[:, t:t + 1], axis=0),
                ).then_inc(fm_rows_in, 16)
            for p in range(2):
                pool.wait_ge(user_in[p], 16 * TILES // 2)
            pool.wait_ge(fm_taken, LOOP_STEPS + 1)
            nc.gpsimd.tensor_tensor(out=fm_total[:, 0:TAIL, :], in0=fm_sum[:, 0:TAIL, :],
                                    in1=user_rows[:, 0:TAIL, :], op=ALU.add).then_inc(totals_ready, 1)
            pool.wait_ge(totals_ready, 1)
            nc.gpsimd.tensor_tensor(out=fm_sq[:, 0:TAIL, :], in0=fm_total[:, 0:TAIL, :],
                                    in1=fm_total[:, 0:TAIL, :], op=ALU.mult).then_inc(squares_ready, 1)
            for g in range(LOOP_STEPS, GROUPS):
                pool.wait_ge(fm_taken, g + 2)
                nc.gpsimd.tensor_tensor(out=fm_total[:, tiles(g), :], in0=fm_sum[:, tiles(g), :],
                                        in1=user_rows[:, tiles(g), :], op=ALU.add).then_inc(totals_ready, 1)

        @block.scalar
        def _(act):
            def scale_split(g, parity):
                nc.scalar.activation(r(sc_hi[:, parity, :]), scale_b[:, cols(g)], ACT.Copy)
                nc.scalar.mul(sc_raw[:, parity, :], scale_b[:, cols(g)],
                              consts[0:ROWS_X, 2:3]).then_inc(scale_parts, 1)

            def pad_copy(g, parity):
                act.wait_ge(user_in[parity], pad_level(g, parity))
                nc.scalar.activation(user_pad[:, parity, :, EMB:P], user_rows[:, tiles(g), :],
                                     ACT.Copy).then_inc(pad_ready, 1)

            def visual_hi(g, parity):
                nc.scalar.activation(r(vis_hi[:, parity, :, :]), vis_in[:, :, cols(g)],
                                     ACT.Copy).then_inc(vis_hi_done, 1)

            def inputs_hi(g, parity):
                act.wait_ge(xa_ready, g + 1)
                nc.scalar.activation(r(xa_hi[0:EMB, parity, :]), projected, ACT.Identity,
                                     bias=visb[0:EMB, 0:1])
                nc.scalar.activation(r(xa_hi[EMB:P, parity, :]), transposed,
                                     ACT.Copy).then_inc(xa_hi_done, 1)

            def fm_scale(g, parity):
                act.wait_ge(fm_ready, g + 1)
                ps = ps_fm[:, 0:TILES_PER_GROUP * FM_COLS].rearrange("p (t c) -> p t c", c=FM_COLS)
                nc.scalar.activation(fm_small[:, tiles(g), :], ps[:, :, 2 * EMB:FM_COLS], ACT.Copy)
                for t in range(TILES_PER_GROUP):
                    last = nc.scalar.activation(face_scaled[:, parity, t, :], ps[:, t, EMB:2 * EMB], ACT.Copy,
                                                scale=scale_c[:, bass.ds(g * TILES_PER_GROUP + t, 1)])
                last.then_inc(fm_face_done, 1)

            def norms_of(rows, norm, g, sink, done, done_before):
                act.wait_ge(done, done_before)
                for t in range(TILES_PER_GROUP):
                    last = nc.scalar.activation(square_sink[:, sink + t, :],
                                                rows[:, bass.ds(g * TILES_PER_GROUP + t, 1), :], ACT.Square,
                                                accum_out=norm[:, bass.ds(g * TILES_PER_GROUP + t, 1)])
                last.then_inc(done, 1)

            def pad_level(g, parity):
                return (g - parity) * (16 * TILES_PER_GROUP // 2) + 16 * TILES_PER_GROUP

            act.wait_ge(early_in, 16)
            nc.scalar.activation(fold_t[EMB:P, 0, :], fold_t[EMB:P, 0, :], ACT.Tanh)
            nc.scalar.activation(fold_t[:, 1, :], fold_t[:, 1, :], ACT.Tanh).then_inc(tables_tanh, 1)
            act.wait_ge(first_in, 16)
            scale_split(0, 0)
            act.wait_ge(late_in, 16)
            nc.scalar.activation(r(visw_hi[:]), visw, ACT.Copy).then_inc(visw_hi_done, 1)
            act.wait_ge(vis_first_in, 16)
            visual_hi(0, 0)
            act.wait_ge(tab_in, 16)
            nc.scalar.activation(tab[:, EMB:2 * EMB], tab[:, EMB:2 * EMB], ACT.Tanh).then_inc(act_step, 1)
            act.wait_ge(act_step, 1)
            nc.scalar.activation(norm_sink[:, 0, :], tab[:, 0:EMB], ACT.Square,
                                 accum_out=tab[:, 2 * EMB + 2:2 * EMB + 3])
            nc.scalar.activation(norm_sink[:, 1, :], tab[:, EMB:2 * EMB], ACT.Square,
                                 accum_out=tab[:, 2 * EMB + 3:2 * EMB + 4]).then_inc(act_step, 1)
            act.wait_ge(act_step, 2)
            nc.scalar.activation(r(tab_hi[:]), tab[:], ACT.Copy).then_inc(tab_hi_done, 1)
            act.wait_ge(fold_done, 1)
            nc.scalar.activation(r(fold_hi[:]), ps_l2[0][0:ROWS_X, :], ACT.Copy).then_inc(fold_hi_done, 1)
            act.wait_ge(pad_zeroed, 1)
            pad_copy(0, 0)
            act.wait_ge(w1_in, 16)
            nc.scalar.activation(r(w1_hi[:]), w1_raw[:], ACT.Copy).then_inc(w1_hi_done, 1)

            def w2_split(k):
                nc.scalar.activation(r(w2_hi[:, k, :]), w2_raw[:, k, :], ACT.Copy).then_inc(w2_hi_done, 1)

            def hidden_hi_half(g, parity, j):
                act.wait_ge(h_ready, g * 2 + j + 1)
                nc.scalar.activation(r(h_hi[:, parity, 2 * j:2 * j + 2, :]), ps_h[j][:],
                                     ACT.Relu).then_inc(h_hi_done, 1)

            def hidden_hi(g, parity):
                hidden_hi_half(g, parity, 0)
                hidden_hi_half(g, parity, 1)

            act.wait_ge(vis_second_in, 16)
            visual_hi(1, 1)
            inputs_hi(0, 0)
            act.wait_ge(w2_in[0], 16)
            w2_split(0)
            w2_split(1)
            act.wait_ge(w2_in[1], 16)
            w2_split(2)
            pad_copy(1, 1)
            hidden_hi_half(0, 0, 0)
            w2_split(3)
            hidden_hi_half(0, 0, 1)
            act.wait_ge(second_in, 16)
            scale_split(1, 1)
            act.wait_ge(scale_c_in, 16)

            def step(g, parity, codes_ahead):
                nxt = 1 - parity
                inputs_hi(g + 1, nxt)
                if codes_ahead:
                    act.wait_ge(vis_rest_in, (g - parity) * 8 + 16)
                    visual_hi(g + 2, parity)
                    act.wait_ge(rest_in, (g - parity) * 8 + 16)
                    act.wait_ge(scale_merged, g + 1)
                    scale_split(g + 2, parity)
                    fm_scale(g, parity)
                    pad_copy(g + 2, parity)
                else:
                    fm_scale(g, parity)
                    for n in range(2):
                        norms_of(user_rows, user_norm, n, 0, user_norm_done, GROUPS - 2 + n)
                    fm_scale(g + 1, nxt)
                hidden_hi(g + 1, nxt)
                if codes_ahead:
                    norms_of(user_rows, user_norm, g + 2, 0, user_norm_done, g)

            with act.Fori(0, LOOP_STEPS // 2) as i:
                for parity in range(2):
                    step(i * 2 + parity, parity, True)
            step(GROUPS - 2, 0, False)
            for n, g in enumerate(range(LOOP_STEPS, GROUPS)):
                act.wait_ge(totals_ready, n + 2)
                norms_of(fm_total, sum_sq, g, 2, sum_sq_done, n)
            act.wait_ge(logits_shifted, 1)
            nc.scalar.activation(expd[:], shifted[:], ACT.Exp).then_inc(exp_done, 1)

        @block.vector
        def _(dve):
            linked = [0]

            def link(ins):
                linked[0] += 1
                ins.then_inc(dve_step, 1)
                dve.wait_ge(dve_step, linked[0])

            nc.vector.memset(warm[:], 0.0).then_inc(warm_zeroed, 1)
            dve.wait_ge(ids_in, 16)
            for n, (size, idx, ready) in enumerate(((USERS, emb_idx, emb_idx_ready), (VOCAB, fm_idx, fm_idx_ready))):
                link(nc.vector.tensor_scalar(id_neg[:, n, :], ids[:], 0.0, float(size), ALU.is_lt, ALU.mult))
                link(nc.vector.tensor_tensor(id_wrap[:, n, :], id_neg[:, n, :], ids[:], ALU.add))
                nc.vector.tensor_scalar(idx[:], id_wrap[:, n, :], 0.0, float(size - 1), ALU.max,
                                        ALU.min).then_inc(ready, 1)
            nc.vector.memset(inv[:], 0.0).then_inc(l2_free, 4)
            nc.vector.memset(denom[:], 0.0).then_inc(dots_done, 4)
            nc.vector.memset(top[:], 0.0).then_inc(fm_taken, 1)

            def make_hots(g, parity):
                dve.wait_ge(scale_parts, g + 1)
                nc.vector.scalar_tensor_tensor(out=sc_part[:, parity, :], in0=sc_hi[:, parity, :],
                                               scalar=consts[0:ROWS_X, 1:2], in1=sc_raw[:, parity, :],
                                               op0=ALU.mult, op1=ALU.add).then_inc(scale_merged, 1)
                nc.vector.tensor_scalar(r(hot[:, parity, :]), codes[0:ROWS_A, cols(g)],
                                        consts[0:ROWS_A, 0:1], None, ALU.is_equal)
                dve.wait_ge(scale_merged, g + 1)
                nc.vector.scalar_tensor_tensor(out=r(hot_scaled[:, parity, :]), in0=codes[:, cols(g)],
                                               scalar=consts[0:ROWS_X, 0:1], in1=sc_part[:, parity, :],
                                               op0=ALU.is_equal, op1=ALU.mult).then_inc(hots_ready, 1)

            def visual_lo(g, parity):
                dve.wait_ge(vis_hi_done, g + 1)
                nc.vector.tensor_tensor(r(vis_lo[:, parity, :, :]), vis_in[:, :, cols(g)],
                                        vis_hi[:, parity, :, :], ALU.subtract).then_inc(vis_lo_done, 1)

            def inputs_lo(g, parity):
                dve.wait_ge(xa_hi_done, g + 1)
                nc.vector.scalar_tensor_tensor(out=r(xa_lo[0:EMB, parity, :]), in0=projected,
                                               scalar=visb[0:EMB, 0:1], in1=xa_hi[0:EMB, parity, :],
                                               op0=ALU.add, op1=ALU.subtract)
                nc.vector.tensor_tensor(r(xa_lo[EMB:P, parity, :]), transposed, xa_hi[EMB:P, parity, :],
                                        ALU.subtract).then_inc(xa_lo_done, 1)

            def hidden_lo_half(g, parity, j):
                dve.wait_ge(h_hi_done, g * 2 + j + 1)
                nc.vector.scalar_tensor_tensor(out=r(h_lo[:, parity, 2 * j:2 * j + 2, :]), in0=ps_h[j][:],
                                               scalar=0.0, in1=h_hi[:, parity, 2 * j:2 * j + 2, :],
                                               op0=ALU.max, op1=ALU.subtract).then_inc(h_lo_done, 1)

            def hidden_lo(g, parity):
                hidden_lo_half(g, parity, 0)
                hidden_lo_half(g, parity, 1)

            def fm_take(g, parity):
                dve.wait_ge(fm_face_done, g + 1)
                ps = ps_fm[:, 0:TILES_PER_GROUP * FM_COLS].rearrange("p (t c) -> p t c", c=FM_COLS)
                nc.vector.tensor_tensor(out=fm_sum[:, tiles(g), :], in0=ps[:, :, 0:EMB],
                                        in1=face_scaled[:, parity, :, :], op=ALU.add).then_inc(fm_taken, 1)

            def output_dots(g, parity, t):
                slot = 2 * parity + t
                dve.wait_ge(l2_ready, g * 2 + t + 1)
                dve.wait_ge(dots_done, g * 2 + t + 1)
                nc.vector.tensor_tensor(out=hidden2[:, slot, :], in0=ps_l2[slot][:], in1=b2_b,
                                        op=ALU.add).then_inc(l2_free, 1)
                dve.wait_ge(l2_free, g * 2 + t + 5)
                for j in range(2):
                    last = nc.vector.scalar_tensor_tensor(
                        out=dot_sink[:, slot, j, :], in0=hidden2[:, slot, :], scalar=0.0, in1=w3_b[:, j, :],
                        op0=ALU.max, op1=ALU.mult, accum_out=mlp[:, bass.ds(g * 2 + t, 1), j])
                last.then_inc(dots_done, 1)

            dve.wait_ge(first_in, 16)
            make_hots(0, 0)
            dve.wait_ge(visw_hi_done, 1)
            nc.vector.tensor_tensor(r(visw_lo[:]), visw, visw_hi[:], ALU.subtract).then_inc(visw_lo_done, 1)
            visual_lo(0, 0)
            dve.wait_ge(tab_hi_done, 1)
            nc.vector.tensor_tensor(r(tab_lo[:]), tab[:], tab_hi[:], ALU.subtract).then_inc(tab_lo_done, 1)
            dve.wait_ge(fold_hi_done, 1)
            nc.vector.tensor_tensor(r(fold_lo[:]), ps_l2[0][0:ROWS_X, :], fold_hi[:],
                                    ALU.subtract).then_inc(fold_lo_done, 1)
            dve.wait_ge(w1_hi_done, 1)
            nc.vector.tensor_tensor(r(w1_lo[:]), w1_raw[:], w1_hi[:], ALU.subtract).then_inc(w1_lo_done, 1)

            def w2_rest(k):
                dve.wait_ge(w2_hi_done, k + 1)
                nc.vector.tensor_tensor(r(w2_lo[:, k, :]), w2_raw[:, k, :], w2_hi[:, k, :],
                                        ALU.subtract).then_inc(w2_lo_done, 1)

            visual_lo(1, 1)
            inputs_lo(0, 0)
            w2_rest(1)
            w2_rest(2)
            hidden_lo_half(0, 0, 0)
            w2_rest(3)
            dve.wait_ge(w2_lo_done, KT - 1)
            hidden_lo_half(0, 0, 1)
            dve.wait_ge(second_in, 16)
            make_hots(1, 1)
            dve.wait_ge(scale_c_in, 16)
            dve.wait_ge(out_rows_in, 16)

            def step(g, parity):
                nxt = 1 - parity
                inputs_lo(g + 1, nxt)
                output_dots(g, parity, 0)
                visual_lo(g + 2, parity)
                fm_take(g, parity)
                dve.wait_ge(rest_in, (g - parity) * 8 + 16)
                make_hots(g + 2, parity)
                hidden_lo(g + 1, nxt)
                output_dots(g, parity, 1)

            with dve.Fori(0, LOOP_STEPS // 2) as i:
                for parity in range(2):
                    step(i * 2 + parity, parity)
            inputs_lo(GROUPS - 1, 1)
            fm_take(GROUPS - 2, 0)
            dve.wait_ge(squares_ready, 1)
            link(nc.vector.reduce_sum(sum_sq[:, 0:TAIL], fm_sq[:, 0:TAIL, :], axis=AX))
            output_dots(GROUPS - 2, 0, 0)
            fm_take(GROUPS - 1, 1)
            hidden_lo(GROUPS - 1, 1)
            nc.vector.tensor_tensor(scale2[:], scale_c[:], scale_c[:], ALU.mult)
            dve.wait_ge(fm_rows_in, 16 * TILES)
            nc.vector.tensor_tensor(base_lin[:], fm_small[:, :, 0:2], fm_rows[:], ALU.add)
            dve.wait_ge(user_norm_done, GROUPS)
            link(nc.vector.tensor_tensor(norms[:, 0, :], user_norm[:], fm_small[:, :, 2], ALU.add))
            link(nc.vector.tensor_tensor(norms[:, 1, :], scale2[:], fm_small[:, :, 3], ALU.mult))
            link(nc.vector.tensor_tensor(norms[:, 2, :], norms[:, 0, :], norms[:, 1, :], ALU.add))
            dve.wait_ge(sum_sq_done, 2)
            link(nc.vector.tensor_tensor(norms[:, 3, :], sum_sq[:], norms[:, 2, :], ALU.subtract))
            for j in range(2):
                last = nc.vector.scalar_tensor_tensor(out=base[:, :, j], in0=norms[:, 3, :], scalar=0.5,
                                                      in1=base_lin[:, :, j], op0=ALU.mult, op1=ALU.add)
            last.then_inc(base_done, 1)
            output_dots(GROUPS - 2, 0, 1)
            for n in range(4):
                t, half = divmod(n, 2)
                hc = slice(half * HALF, (half + 1) * HALF)
                dve.wait_ge(l2_ready, TILES - 2 + n + 1)
                nc.vector.tensor_tensor(out=hidden2[:, 2 + t, hc], in0=tail_bank(n)[:, 0:HALF],
                                        in1=b2_b[:, hc], op=ALU.add).then_inc(l2_free, 1)
                if n == 3:
                    dve.wait_ge(halves_done, 3)
                    dve.wait_ge(base_done, 1)
                    nc.vector.tensor_tensor(base[:, TILES - 2:TILES, :], base[:, TILES - 2:TILES, :],
                                            tail_dots[:], ALU.add).then_inc(base_done, 1)
                dve.wait_ge(l2_free, 4 + TILES - 2 + n + 1)
                for j in range(2):
                    tile = TILES - 2 + t
                    last = nc.vector.scalar_tensor_tensor(
                        out=dot_sink[:, 2 + t, j, hc], in0=hidden2[:, 2 + t, hc], scalar=0.0, in1=w3_b[:, j, hc],
                        op0=ALU.max, op1=ALU.mult,
                        accum_out=(mlp[:, tile, j:j + 1] if half else tail_dots[:, t, j:j + 1]))
                last.then_inc(halves_done, 1)

            dve.wait_ge(dots_done, 4 + TILES - 2)
            dve.wait_ge(halves_done, 4)
            dve.wait_ge(base_done, 2)
            link(nc.vector.tensor_tensor(logits[:], mlp[:], base[:], ALU.add))
            link(nc.vector.tensor_tensor(top[:], logits[:, :, 0], logits[:, :, 1], ALU.max))
            both = lambda x: x[:].rearrange("p (t a) -> p t a", a=1).to_broadcast([P, TILES, 2])
            nc.vector.tensor_tensor(shifted[:], logits[:], both(top), ALU.subtract).then_inc(logits_shifted, 1)
            dve.wait_ge(exp_done, 1)
            link(nc.vector.tensor_tensor(denom[:], expd[:, :, 0], expd[:, :, 1], ALU.add))
            link(nc.vector.reciprocal(inv[:], denom[:]))
            nc.vector.tensor_tensor(probs[:], expd[:], both(inv), ALU.mult).then_inc(probs_done, 1)

        @block.tensor
        def _(pe):
            def front(g, parity):
                pe.wait_ge(pad_ready, g + 1)
                for t in range(TILES_PER_GROUP):
                    nc.tensor.transpose(ps_xa[:, GROUP + t * P:GROUP + (t + 1) * P], user_pad[:, parity, t, :],
                                        ident[:])
                pe.wait_ge(vis_lo_done, g + 1)
                passes = [(w, x, k) for w, x in ((visw_hi, vis_hi), (visw_lo, vis_hi), (visw_hi, vis_lo))
                          for k in range(2)]
                for n, (w, x, k) in enumerate(passes):
                    last = nc.tensor.matmul(ps_xa[:, 0:GROUP], r(w[:, k, :]), r(x[:, parity, k, :]),
                                            start=(n == 0), stop=(n == len(passes) - 1))
                last.then_inc(xa_ready, 1)

            def layer1_tables(m, parity, start=True):
                o = ps_h[m // 2][:, m % 2, :]
                mc = slice(m * P, (m + 1) * P)
                nc.tensor.matmul(o, r(fold_hi[:, mc]), r(hot_scaled[:, parity, :]), start=start, stop=False)
                nc.tensor.matmul(o, r(fold_lo[0:ROWS_A, mc]), r(hot_scaled[0:ROWS_A, parity, :]),
                                 start=False, stop=False)

            def layer1_hi(m, parity):
                o = ps_h[m // 2][:, m % 2, :]
                mc = slice(m * P, (m + 1) * P)
                nc.tensor.matmul(o, r(w1_hi[:, mc]), r(xa_hi[:, parity, :]), start=False, stop=False)
                nc.tensor.matmul(o, r(w1_lo[:, mc]), r(xa_hi[:, parity, :]), start=False, stop=False)

            def layer1_lo(m, parity, stop=True):
                last = nc.tensor.matmul(ps_h[m // 2][:, m % 2, :], r(w1_hi[:, m * P:(m + 1) * P]),
                                        r(xa_lo[:, parity, :]), start=False, stop=stop)
                if m % 2 == 1:
                    last.then_inc(h_ready, 1)

            def layer1(g, parity):
                pe.wait_ge(hots_ready, g + 1)
                pe.wait_ge(xa_lo_done, g + 1)
                for m in range(KT):
                    layer1_tables(m, parity)
                    layer1_hi(m, parity)
                    layer1_lo(m, parity)

            def lookups(g, parity):
                pe.wait_ge(tab_lo_done, 1)
                pe.wait_ge(hots_ready, g + 1)
                pe.wait_ge(fm_taken, g + 1)
                for t in range(TILES_PER_GROUP):
                    o = ps_fm[:, t * FM_COLS:(t + 1) * FM_COLS]
                    h = r(hot[:, parity, t * P:(t + 1) * P])
                    nc.tensor.matmul(o, h, r(tab_hi[:]), start=True, stop=False)
                    last = nc.tensor.matmul(o, h, r(tab_lo[:]), start=False, stop=True)
                last.then_inc(fm_ready, 1)

            def layer2(g, parity, t):
                pe.wait_ge(l2_free, g * 2 + t + 1)
                o = ps_l2[2 * parity + t][:]
                tc = slice(t * P, (t + 1) * P)
                for k in range(KT):
                    if t == 0 and k % 2 == 0:
                        pe.wait_ge(h_lo_done, g * 2 + k // 2 + 1)
                    hi = r(h_hi[:, parity, k, tc])
                    lo = r(h_lo[:, parity, k, tc])
                    nc.tensor.matmul(o, hi, r(w2_hi[:, k, :]), start=(k == 0), stop=False)
                    nc.tensor.matmul(o, hi, r(w2_lo[:, k, :]), start=False, stop=False)
                    last = nc.tensor.matmul(o, lo, r(w2_hi[:, k, :]), start=False, stop=(k == KT - 1))
                last.then_inc(l2_ready, 1)

            def keep_warm(count):
                for _ in range(count):
                    nc.tensor.matmul(ps_l2[3][:], warm[:, 0:P], warm[:], start=True, stop=True)

            pe.wait_ge(warm_zeroed, 1)
            keep_warm(WARM_UP[0])
            pe.wait_ge(tables_tanh, 1)
            pe.wait_ge(fold_in, 16)
            o = ps_l2[0][0:ROWS_X, :]
            for n in range(2):
                nc.tensor.matmul(o, fold_t[:, n, :], fold_w_sb[:, n, :], start=(n == 0), stop=False)
            pe.wait_ge(b1_in, 16)
            nc.tensor.matmul(o, b1_sb[:, HIDDEN:HIDDEN + ROWS_X], b1_sb[:, 0:HIDDEN], start=False,
                             stop=True).then_inc(fold_done, 1)
            keep_warm(WARM_UP[1])
            pe.wait_ge(late_in, 16)
            pe.wait_ge(visw_lo_done, 1)
            front(0, 0)
            pe.wait_ge(fold_lo_done, 1)
            pe.wait_ge(hots_ready, 1)
            for m in range(KT):
                layer1_tables(m, 0, start=(m % 2 == 0))
            pe.wait_ge(w1_lo_done, 1)
            pe.wait_ge(xa_hi_done, 1)
            for m in range(KT):
                layer1_hi(m, 0)
            pe.wait_ge(xa_lo_done, 1)
            for m in range(KT):
                layer1_lo(m, 0, stop=(m % 2 == 1))
            keep_warm(WARM_UP[2])
            front(1, 1)

            def step(g, parity):
                layer2(g, parity, 0)
                lookups(g, parity)
                layer1(g + 1, 1 - parity)
                layer2(g, parity, 1)
                front(g + 2, parity)

            pe.wait_ge(w2_first_lo_done, 1)
            pe.wait_ge(w2_lo_done, 1)
            with pe.Fori(0, LOOP_STEPS // 2) as i:
                for parity in range(2):
                    step(i * 2 + parity, parity)
            lookups(GROUPS - 2, 0)
            layer2(GROUPS - 2, 0, 0)
            lookups(GROUPS - 1, 1)
            layer1(GROUPS - 1, 1)
            layer2(GROUPS - 2, 0, 1)
            pe.wait_ge(l2_free, TILES)
            for n in range(4):
                t, half = divmod(n, 2)
                if n == 1:
                    pe.wait_ge(l2_free, TILES - 2 + 4)
                tc = slice(t * P, (t + 1) * P)
                hc = slice(half * HALF, (half + 1) * HALF)
                o = tail_bank(n)[:, 0:HALF]
                for k in range(KT):
                    if n == 0 and k % 2 == 0:
                        pe.wait_ge(h_lo_done, (GROUPS - 1) * 2 + k // 2 + 1)
                    hi = r(h_hi[:, 1, k, tc])
                    nc.tensor.matmul(o, hi, r(w2_hi[:, k, hc]), start=(k == 0), stop=False)
                    nc.tensor.matmul(o, hi, r(w2_lo[:, k, hc]), start=False, stop=False)
                    last = nc.tensor.matmul(o, r(h_lo[:, 1, k, tc]), r(w2_hi[:, k, hc]), start=False,
                                            stop=(k == KT - 1))
                last.then_inc(l2_ready, 1)


def kernel(r_visual, r_user_id, r_hour, r_scale, r_gender, r_age, r_attribute, L0_rec_user_emb,
           L0_rec_hour_emb, L0_rec_gender_emb, L0_rec_age_emb, L0_rec_attr_emb, L0_rec_visu_w,
           L0_rec_visu_b, L0_rec_fm_w, L0_rec_fm_b, L0_rec_w1, L0_rec_b1, L0_rec_w2, L0_rec_b2,
           L0_rec_w3, L0_rec_b3):
    import numpy as np
    import concourse.bacc as bacc
    from concourse.bass_utils import run_bass_kernel_spmd

    f32 = np.float32
    visual = np.asarray(r_visual).T.reshape(2, P, ROWS).transpose(1, 0, 2)
    by_tile = lambda a: np.asarray(a).reshape(TILES, P).T

    ids = [np.asarray(a)[None, :] for a in (r_hour, r_gender, r_age, r_attribute)]
    repeated = [np.repeat(a, n, axis=0) for a, n in zip(ids, FIELD_SIZES)]
    code_rows = np.concatenate(repeated + [np.zeros((BIAS_ROWS, ROWS), ids[0].dtype)] + repeated[1:])
    scale = np.asarray(r_scale).reshape(1, ROWS)
    scale_rows = np.concatenate([np.ones((FIELD_SIZES[0], ROWS), f32), np.repeat(scale, ROWS_B, axis=0),
                                 np.ones((BIAS_ROWS, ROWS), f32), np.repeat(scale, ROWS_B, axis=0)])
    lookup_inputs = np.stack([code_rows, scale_rows.view(np.int32)], axis=1)

    numbers = [np.arange(n) for n in FIELD_SIZES]
    consts = np.zeros((P, CONST_COLS), f32)
    consts[0:ROWS_X, 0] = np.concatenate(numbers + [np.zeros(BIAS_ROWS)] + numbers[1:])
    consts[0:ROWS_A, 1] = 1.0
    consts[ROWS_A:ROWS_X, 1] = -1.0
    consts[ROWS_A:ROWS_X, 2] = 1.0

    w1t = np.asarray(L0_rec_w1).T
    user_w, hour_w, gender_w, attr_w, age_w, vis_w = (w1t[n * EMB:(n + 1) * EMB] for n in range(6))
    fold_w = np.stack([np.concatenate([hour_w, age_w]), np.concatenate([gender_w, attr_w])], axis=1)
    hour, gender, age, attr = (np.asarray(a) for a in (L0_rec_hour_emb, L0_rec_gender_emb,
                                                       L0_rec_age_emb, L0_rec_attr_emb))
    starts = np.cumsum((0,) + FIELD_SIZES)
    fold_tables = np.zeros((P, 2, ROWS_X), f32)
    lookup_tables = np.zeros((ROWS_A, 2 * EMB + 2), f32)
    for n, (table, top, pair) in enumerate(((hour, 0, 0), (gender, 0, 1), (age, EMB, 0), (attr, EMB, 1))):
        at = starts[n]
        fold_tables[top:top + EMB, pair, at:at + len(table)] = table.T
        lookup_tables[at:at + len(table), min(n, 1) * EMB:(min(n, 1) + 1) * EMB] = table
        if n:
            at += ROWS_A - FIELD_SIZES[0]
            fold_tables[top:top + EMB, pair, at:at + len(table)] = table.T
    fm_rows = np.asarray(L0_rec_fm_w).T
    lookup_tables[0:LOOKUP, 2 * EMB:] = fm_rows[USERS:]
    lookup_tables[LOOKUP, 2 * EMB:] = L0_rec_fm_b
    lookup_tables[LOOKUP + 1, 2 * EMB:] = L0_rec_b3
    b1_row = np.zeros((1, HIDDEN + ROWS_X), f32)
    b1_row[0, 0:HIDDEN] = L0_rec_b1
    b1_row[0, HIDDEN + LOOKUP] = 1.0
    visu_w = np.zeros((P, 2, P), f32)
    visu_w[:, :, 0:EMB] = np.asarray(L0_rec_visu_w).T.reshape(2, P, EMB).transpose(1, 0, 2)
    visu_b = np.concatenate([np.asarray(L0_rec_visu_b), np.zeros(EMB, f32)])[:, None]

    arrays = {
        "visual": visual,
        "user_ids": by_tile(r_user_id),
        "lookup_inputs": lookup_inputs,
        "scale_cols": by_tile(r_scale),
        "user_emb": L0_rec_user_emb,
        "fm_user": fm_rows,
        "hidden1_w": np.concatenate([vis_w, user_w]),
        "fold_w": fold_w,
        "small_early": np.concatenate([fold_tables.reshape(P, -1), consts], axis=1),
        "small_late": np.concatenate([visu_w.reshape(P, -1), visu_b, np.eye(P, dtype=f32)], axis=1),
        "b1_row": b1_row,
        "lookup_tables": lookup_tables,
        "w2": np.asarray(L0_rec_w2).T.reshape(KT, P, HIDDEN).transpose(1, 0, 2),
        "out_rows": np.concatenate([np.asarray(L0_rec_b2)[None, :], L0_rec_w3]),
    }
    arrays = {name: np.ascontiguousarray(a) for name, a in arrays.items()}
    nc = bacc.Bacc("TRN2", target_bir_lowering=False, num_devices=1)
    aps = [nc.dram_tensor(name, a.shape, mybir.dt.from_np(a.dtype), kind="ExternalInput").ap()
           for name, a in arrays.items()]
    out = nc.dram_tensor("out", (P, TILES, 2), mybir.dt.float32, kind="ExternalOutput").ap()
    rec_program(nc, *aps, out)
    result = run_bass_kernel_spmd(nc, [arrays], core_ids=[0])
    return result.results[0]["out"].transpose(1, 0, 2).reshape(ROWS, 2)
```
